# Optimizing a Trainium2 kernel written in Bass

```python
import numpy as np
import jax
import jax.numpy as jnp

def _softmax(x, axis=-1):
    return jax.nn.softmax(x, axis=axis)

def _gelu(x):
    return jax.nn.gelu(x, approximate=True)

def _silu(x):
    return jax.nn.silu(x)

def _sigmoid(x):
    return jax.nn.sigmoid(x)

def _layernorm(x, axis=-1, eps=1e-05):
    m = jnp.mean(x, axis=axis, keepdims=True)
    v = jnp.var(x, axis=axis, keepdims=True)
    return (x - m) / jnp.sqrt(v + eps)

def _scatter_add(tgt, idx, src, axis=0):
    return tgt.at[idx].add(src)

def _segment_sum(src, seg, n):
    return jax.ops.segment_sum(src, seg, n)
kernel_name = 'mk_gps_d1_gnn_r8_fb4ffe'

def setup_inputs(seed: int=0):
    np.random.seed(seed)
    _w = jnp.asarray

    def _rec_inputs():
        import jax
        import jax.numpy as jnp
        _gk = jax.random.key(seed)
        x = -0.0003713 + 1 * jax.random.normal(jax.random.fold_in(_gk, 1), (6250, 256), jnp.float32)
        _s = jax.random.randint(jax.random.fold_in(_gk, 2), (50000,), 0, 6250, jnp.int32)
        _d = jax.random.randint(jax.random.fold_in(_gk, 3), (50000,), 0, 6250, jnp.int32)
        _loop = jnp.arange(6250, dtype=jnp.int32)
        src = jnp.concatenate([_s, _d, _loop])
        dst = jnp.concatenate([_d, _s, _loop])
        _o = jnp.argsort(dst, stable=True)
        src = src[_o]
        dst = dst[_o]
        return (x, src, dst)
    x, src, dst = _rec_inputs()

    def _L0_gnn_setup():
        import jax, jax.numpy as jnp
        import numpy as np
        N_NODES = 6250
        N_EDGES = 100000
        D = 256
        key = jax.random.key(seed)
        k_x, k_e, k_w1, k_w2 = jax.random.split(key, 4)
        x = jax.random.normal(k_x, (N_NODES, D), dtype=jnp.float32)
        edge_index = jax.random.randint(k_e, (2, N_EDGES), 0, N_NODES, dtype=jnp.int64)
        W1 = jax.random.normal(k_w1, (D, D // 2), dtype=jnp.float32) * (1.0 / np.sqrt(D))
        b1 = jnp.zeros((D // 2,), dtype=jnp.float32)
        W2 = jax.random.normal(k_w2, (D // 2, 1), dtype=jnp.float32) * (1.0 / np.sqrt(D // 2))
        b2 = jnp.zeros((1,), dtype=jnp.float32)
        return {'x': x, 'edge_index': edge_index, 'W1': W1, 'b1': b1, 'W2': W2, 'b2': b2}
    _L0_gnn_all = _L0_gnn_setup()
    _L0_gnn_in = {k: v for k, v in _L0_gnn_all.items() if k in ('W1', 'b1', 'W2', 'b2')}
    del _L0_gnn_all

    def _L0_mix_setup():
        import jax, jax.numpy as jnp
        import numpy as np
        D_MODEL = 256
        NUM_HEADS = 8
        DEPTH = D_MODEL // NUM_HEADS
        B, L = (32, 512)

        def _feature_map(x):
            return jax.nn.elu(x) + 1.0
        key = jax.random.key(seed)
        ks = jax.random.split(key, 9)
        sc = 1.0 / np.sqrt(D_MODEL)
        return {'x': jax.random.normal(ks[0], (B, L, D_MODEL), dtype=jnp.float32), 'wq': jax.random.normal(ks[1], (D_MODEL, D_MODEL), dtype=jnp.float32) * sc, 'bq': jnp.zeros((D_MODEL,), dtype=jnp.float32), 'wk': jax.random.normal(ks[2], (D_MODEL, D_MODEL), dtype=jnp.float32) * sc, 'bk': jnp.zeros((D_MODEL,), dtype=jnp.float32), 'wv': jax.random.normal(ks[3], (D_MODEL, D_MODEL), dtype=jnp.float32) * sc, 'bv': jnp.zeros((D_MODEL,), dtype=jnp.float32), 'wo': jax.random.normal(ks[4], (D_MODEL, D_MODEL), dtype=jnp.float32) * sc, 'bo': jnp.zeros((D_MODEL,), dtype=jnp.float32)}
    _L0_mix_all = _L0_mix_setup()
    _L0_mix_in = {k: v for k, v in _L0_mix_all.items() if k in ('wq', 'bq', 'wk', 'bk', 'wv', 'bv', 'wo', 'bo')}
    del _L0_mix_all

    def _L0_ffn_setup():
        import jax, jax.numpy as jnp
        import numpy as np
        B, N, D = (16, 512, 256)
        NUM_EXPERTS, TOP_K, HEADS = (4, 2, 4)
        N_EDGES = 131072
        LN_EPS = 1e-05

        def _layernorm(x, g, b):
            mu = x.mean(-1, keepdims=True)
            var = ((x - mu) ** 2).mean(-1, keepdims=True)
            return (x - mu) * jax.lax.rsqrt(var + LN_EPS) * g + b

        def _forward(x, edge_index, W_gat, att_src, att_dst, b_gat, ln_gamma, ln_beta, W1, b1, W2, b2):
            Bc, Nc, Dc = x.shape
            M = Bc * Nc
            x_flat = x.reshape(M, Dc)
            h = (x_flat @ W_gat).reshape(M, HEADS, NUM_EXPERTS)
            loops = jnp.arange(M, dtype=edge_index.dtype)
            src = jnp.concatenate([edge_index[0], loops])
            dst = jnp.concatenate([edge_index[1], loops])
            a_src = (h * att_src).sum(-1)
            a_dst = (h * att_dst).sum(-1)
            e = jax.nn.leaky_relu(a_src[src] + a_dst[dst], negative_slope=0.2)
            e_max = jax.ops.segment_max(e, dst, num_segments=M)
            ee = jnp.exp(e - e_max[dst])
            denom = jax.ops.segment_sum(ee, dst, num_segments=M)
            alpha = ee / (denom[dst] + 1e-16)
            msg = h[src] * alpha[:, :, None]
            agg = jax.ops.segment_sum(msg, dst, num_segments=M).reshape(M, HEADS * NUM_EXPERTS) + b_gat
            scores = _layernorm(agg, ln_gamma, ln_beta).reshape(M, HEADS, NUM_EXPERTS).mean(1)
            scores = scores.reshape(Bc, Nc, NUM_EXPERTS)
            topk_s, topk_i = jax.lax.top_k(scores, TOP_K)
            w = jax.nn.softmax(topk_s, axis=-1)
            out = jnp.zeros_like(x)
            for ei in range(NUM_EXPERTS):
                g = jnp.where(topk_i == ei, w, 0.0).sum(-1)
                hh = jax.nn.gelu(x @ W1[ei] + b1[ei], approximate=False)
                out = out + g[..., None] * (hh @ W2[ei] + b2[ei])
            return out
        key = jax.random.key(seed)
        ks = jax.random.split(key, 8)
        s = 0.05
        return {'x': jax.random.normal(ks[0], (B, N, D), jnp.float32), 'W_gat': jax.random.normal(ks[1], (D, HEADS * NUM_EXPERTS), jnp.float32) * s, 'att_src': jax.random.normal(ks[2], (HEADS, NUM_EXPERTS), jnp.float32) * s, 'att_dst': jax.random.normal(ks[3], (HEADS, NUM_EXPERTS), jnp.float32) * s, 'b_gat': jnp.zeros((HEADS * NUM_EXPERTS,), jnp.float32), 'ln_gamma': jnp.ones((HEADS * NUM_EXPERTS,), jnp.float32), 'ln_beta': jnp.zeros((HEADS * NUM_EXPERTS,), jnp.float32), 'W1': jax.random.normal(ks[4], (NUM_EXPERTS, D, 2 * D), jnp.float32) * s, 'b1': jnp.zeros((NUM_EXPERTS, 2 * D), jnp.float32), 'W2': jax.random.normal(ks[5], (NUM_EXPERTS, 2 * D, D), jnp.float32) * s, 'b2': jnp.zeros((NUM_EXPERTS, D), jnp.float32), 'edge_index': jax.random.randint(ks[6], (2, N_EDGES), 0, B * N, jnp.int32)}
    _L0_ffn_all = _L0_ffn_setup()
    _L0_ffn_in = {k: v for k, v in _L0_ffn_all.items() if k in ('W_gat', 'att_src', 'att_dst', 'b_gat', 'ln_gamma', 'ln_beta', 'W1', 'b1', 'W2', 'b2', 'edge_index')}
    del _L0_ffn_all
    return {'x': x, 'src': src, 'dst': dst, 'L0_gnn_W1': _L0_gnn_in['W1'], 'L0_gnn_b1': _L0_gnn_in['b1'], 'L0_gnn_W2': _L0_gnn_in['W2'], 'L0_gnn_b2': _L0_gnn_in['b2'], 'L0_mix_wq': _L0_mix_in['wq'], 'L0_mix_bq': _L0_mix_in['bq'], 'L0_mix_wk': _L0_mix_in['wk'], 'L0_mix_bk': _L0_mix_in['bk'], 'L0_mix_wv': _L0_mix_in['wv'], 'L0_mix_bv': _L0_mix_in['bv'], 'L0_mix_wo': _L0_mix_in['wo'], 'L0_mix_bo': _L0_mix_in['bo'], 'L0_ffn_W_gat': _L0_ffn_in['W_gat'], 'L0_ffn_att_src': _L0_ffn_in['att_src'], 'L0_ffn_att_dst': _L0_ffn_in['att_dst'], 'L0_ffn_b_gat': _L0_ffn_in['b_gat'], 'L0_ffn_ln_gamma': _L0_ffn_in['ln_gamma'], 'L0_ffn_ln_beta': _L0_ffn_in['ln_beta'], 'L0_ffn_W1': _L0_ffn_in['W1'], 'L0_ffn_b1': _L0_ffn_in['b1'], 'L0_ffn_W2': _L0_ffn_in['W2'], 'L0_ffn_b2': _L0_ffn_in['b2'], 'L0_ffn_edge_index': _L0_ffn_in['edge_index']}

def reference(x, src, dst, L0_gnn_W1, L0_gnn_b1, L0_gnn_W2, L0_gnn_b2, L0_mix_wq, L0_mix_bq, L0_mix_wk, L0_mix_bk, L0_mix_wv, L0_mix_bv, L0_mix_wo, L0_mix_bo, L0_ffn_W_gat, L0_ffn_att_src, L0_ffn_att_dst, L0_ffn_b_gat, L0_ffn_ln_gamma, L0_ffn_ln_beta, L0_ffn_W1, L0_ffn_b1, L0_ffn_W2, L0_ffn_b2, L0_ffn_edge_index):
    import jax
    import jax.numpy as jnp

    def _L0_gnn_ref(x, edge_index, W1, b1, W2, b2):
        import jax, jax.numpy as jnp
        import numpy as np
        N_NODES = 6250
        N_EDGES = 100000
        D = 256
        row, col = (edge_index[0], edge_index[1])
        neigh = x[col]
        h = jax.nn.relu(neigh @ W1 + b1)
        w = jax.nn.sigmoid(h @ W2 + b2)
        num = jax.ops.segment_sum(neigh * w, row, num_segments=N_NODES)
        den = jax.ops.segment_sum(w, row, num_segments=N_NODES)
        out = jnp.where(den > 0, num / jnp.maximum(den, 1e-12), 0.0)
        return out

    def _L0_mix_ref(x, wq, bq, wk, bk, wv, bv, wo, bo):
        import jax, jax.numpy as jnp
        import numpy as np
        D_MODEL = 256
        NUM_HEADS = 8
        DEPTH = D_MODEL // NUM_HEADS
        B, L = (32, 512)

        def _feature_map(x):
            return jax.nn.elu(x) + 1.0
        b, l, _ = x.shape
        q = (x @ wq + bq).reshape(b, l, NUM_HEADS, DEPTH)
        k = (x @ wk + bk).reshape(b, l, NUM_HEADS, DEPTH)
        v = (x @ wv + bv).reshape(b, l, NUM_HEADS, DEPTH)
        q = _feature_map(q)
        k = _feature_map(k)
        kv = jnp.einsum('blhd,blhe->bhde', k, v)
        k_sum = jnp.sum(k, axis=1)
        qkv = jnp.einsum('blhd,bhde->blhe', q, kv)
        normalizer = jnp.einsum('blhd,bhd->blh', q, k_sum) + 1e-06
        out = qkv / normalizer[..., None]
        out = out.reshape(b, l, D_MODEL)
        return out @ wo + bo

    def _L0_ffn_ref(x, W_gat, att_src, att_dst, b_gat, ln_gamma, ln_beta, W1, b1, W2, b2, edge_index):
        import jax, jax.numpy as jnp
        import numpy as np
        B, N, D = (16, 512, 256)
        NUM_EXPERTS, TOP_K, HEADS = (4, 2, 4)
        N_EDGES = 131072
        LN_EPS = 1e-05

        def _layernorm(x, g, b):
            mu = x.mean(-1, keepdims=True)
            var = ((x - mu) ** 2).mean(-1, keepdims=True)
            return (x - mu) * jax.lax.rsqrt(var + LN_EPS) * g + b

        def _forward(x, edge_index, W_gat, att_src, att_dst, b_gat, ln_gamma, ln_beta, W1, b1, W2, b2):
            Bc, Nc, Dc = x.shape
            M = Bc * Nc
            x_flat = x.reshape(M, Dc)
            h = (x_flat @ W_gat).reshape(M, HEADS, NUM_EXPERTS)
            loops = jnp.arange(M, dtype=edge_index.dtype)
            src = jnp.concatenate([edge_index[0], loops])
            dst = jnp.concatenate([edge_index[1], loops])
            a_src = (h * att_src).sum(-1)
            a_dst = (h * att_dst).sum(-1)
            e = jax.nn.leaky_relu(a_src[src] + a_dst[dst], negative_slope=0.2)
            e_max = jax.ops.segment_max(e, dst, num_segments=M)
            ee = jnp.exp(e - e_max[dst])
            denom = jax.ops.segment_sum(ee, dst, num_segments=M)
            alpha = ee / (denom[dst] + 1e-16)
            msg = h[src] * alpha[:, :, None]
            agg = jax.ops.segment_sum(msg, dst, num_segments=M).reshape(M, HEADS * NUM_EXPERTS) + b_gat
            scores = _layernorm(agg, ln_gamma, ln_beta).reshape(M, HEADS, NUM_EXPERTS).mean(1)
            scores = scores.reshape(Bc, Nc, NUM_EXPERTS)
            topk_s, topk_i = jax.lax.top_k(scores, TOP_K)
            w = jax.nn.softmax(topk_s, axis=-1)
            out = jnp.zeros_like(x)
            for ei in range(NUM_EXPERTS):
                g = jnp.where(topk_i == ei, w, 0.0).sum(-1)
                hh = jax.nn.gelu(x @ W1[ei] + b1[ei], approximate=False)
                out = out + g[..., None] * (hh @ W2[ei] + b2[ei])
            return out
        return _forward(x, edge_index, W_gat, att_src, att_dst, b_gat, ln_gamma, ln_beta, W1, b1, W2, b2)
    edge_index = jnp.stack([src, dst])
    xn = _layernorm(x, axis=-1)
    x = x + _L0_gnn_ref(xn, edge_index, L0_gnn_W1, L0_gnn_b1, L0_gnn_W2, L0_gnn_b2) + _L0_mix_ref(xn[None], L0_mix_wq, L0_mix_bq, L0_mix_wk, L0_mix_bk, L0_mix_wv, L0_mix_bv, L0_mix_wo, L0_mix_bo)[0]
    x = x + _L0_ffn_ref(_layernorm(x, axis=-1)[None], L0_ffn_W_gat, L0_ffn_att_src, L0_ffn_att_dst, L0_ffn_b_gat, L0_ffn_ln_gamma, L0_ffn_ln_beta, L0_ffn_W1, L0_ffn_b1, L0_ffn_W2, L0_ffn_b2, L0_ffn_edge_index)[0]
    return x

_drawn_inputs = setup_inputs


def setup_inputs(seed=0):
    import zlib

    import numpy as np

    out = dict(_drawn_inputs(seed))
    spreads = {'L0_gnn_b1': (0.0, 0.419),
     'L0_mix_bq': (0.0, 2.0),
     'L0_mix_bk': (0.0, 2.0),
     'L0_mix_bv': (0.0, 0.1),
     'L0_mix_bo': (0.0, 0.1),
     'L0_ffn_b_gat': (0.0, 0.1),
     'L0_ffn_ln_gamma': (1.0, 0.2),
     'L0_ffn_ln_beta': (0.0, 0.1),
     'L0_ffn_b1': (0.0, 0.1),
     'L0_ffn_b2': (0.0, 0.1)}
    factors = {'L0_mix_wq': 12.731}
    for name, (base, spread) in spreads.items():
        noise = np.random.default_rng([zlib.crc32(name.encode()), seed]).standard_normal(out[name].shape)
        drawn = base * np.exp(spread * noise) if base else spread * noise
        out[name] = jnp.asarray(drawn.astype(out[name].dtype))
    for name, factor in factors.items():
        out[name] = (out[name] * factor).astype(out[name].dtype)
    return out
```

```python
from contextlib import ExitStack

import concourse.bass as bass
from concourse import mybir

ALU = mybir.AluOpType
ACT = mybir.ActivationFunctionType
AX = mybir.AxisListType
F32 = mybir.dt.float32
I32 = mybir.dt.int32
RED = bass.bass_isa.ReduceOp

P = 128
LN_EPS = 1e-5
FAR = float(1 << 20)


class Steps:

    def __init__(self, eng, sem, base=0):
        self.eng, self.sem, self.n = eng, sem, base

    def did(self, ins):
        ins.then_inc(self.sem, 1)
        self.n = self.n + 1

    def settle(self):
        self.eng.wait_ge(self.sem, self.n)

    def step(self, ins):
        self.did(ins)
        self.settle()


class EdgeList:

    def __init__(self, parts, cols, unroll, blocks, group):
        self.parts, self.cols, self.unroll = parts, cols, unroll
        tiles = (parts * cols + (P - 1) * blocks) // P
        self.tiles = -(-tiles // group) * group
        assert cols % (2 * unroll) == 0


def gps_kernel(nc, x, src, dst, gW1, gb1, gW2, gb2, wq, bq, wk, bk, wv, bv, wo, bo, W_gat, att_src, att_dst,
               b_gat, ln_gamma, ln_beta, fW1, fb1, fW2, fb2, edge_index, out, stop_after=0, debug=None):
    N, D = x.shape
    B = -(-N // P)
    FULL = N // P
    LAST = N - FULL * P
    NP = B * P
    HID = gW1.shape[1]
    YW = D + 1
    HEADS, EXPERTS = att_src.shape
    HE = HEADS * EXPERTS
    RW = 2 * HEADS + HE
    KW = HEADS + HE
    MH = 8
    MD = D // MH
    FH = fW1.shape[2]
    FC = FH // P
    G = 8
    HG = G // 2
    E1 = EdgeList(125, src.shape[0] // 125, 5, B, G)
    E2 = EdgeList(P, edge_index.shape[1] // P, 16, B, G)
    assert 125 * E1.cols == src.shape[0] and P * E2.cols == edge_index.shape[1]
    T1, T2 = E1.tiles, E2.tiles

    ctx = ExitStack()

    def sb(name, shape, dt=F32):
        return ctx.enter_context(nc.sbuf_tensor(name, shape, dt))

    def ps(name, shape, dt=F32):
        return ctx.enter_context(nc.psum_tensor(name, shape, dt))

    def sem(name):
        return ctx.enter_context(nc.semaphore(name))

    def dram(name, shape, dt=F32):
        return nc.dram_tensor(name, shape, dt, kind="Internal").ap()

    list1_dram = dram("list1_dram", [P * T1, 2])
    list2_dram = dram("list2_dram", [P * T2, 2])
    y_dram = dram("y_dram", [NP, YW])
    node_dram = dram("node_dram", [NP, RW])

    res = sb("res", [P, B, D])
    big = sb("big", [P, 2 * B * P + B * YW])
    list1 = sb("list1", [P, T1, 2])
    list2 = sb("list2", [P, T2, 2])
    blk1 = sb("blk1", [1, T1], I32)
    blk2 = sb("blk2", [1, T2], I32)
    ident = sb("ident", [P, P])
    ones = sb("ones", [P, P])
    before = sb("before", [P, P])
    lane = sb("lane", [P, P])
    valid = sb("valid", [P, B])
    epsc = sb("epsc", [P, 1])
    mean = sb("mean", [P, B, 2])
    rstd = sb("rstd", [P, B])
    bst = sb("bst", [P, B, 6])

    zero1, turn = sb("zero1", [1, 1]), sb("turn", [1, 1])
    turned, turns = sem("turned"), [0]
    y_stored, node_stored = sem("y_stored"), sem("node_stored")

    XNT = 2 * B * P
    xnT = big[:, 0:XNT].rearrange("p (c n) -> p c n", c=2)
    acc = big[:, XNT:].rearrange("p (b w) -> p b w", w=YW)
    gat = big[:, 0:T2 * KW].rearrange("p (t w) -> p t w", w=KW)

    with ExitStack() as c1:
        def sb1(name, shape, dt=F32):
            return c1.enter_context(nc.sbuf_tensor(name, shape, dt))

        def ps1(name, shape, dt=F32):
            return c1.enter_context(nc.psum_tensor(name, shape, dt))

        def sem1(name):
            return c1.enter_context(nc.semaphore(name))

        at = [XNT]

        def scratch(*shape):
            n = 1
            for s in shape:
                n *= s
            v = big[:, at[0]:at[0] + n]
            at[0] += n
            assert at[0] <= XNT + B * YW
            return v

        C = max(E1.cols, E2.cols)
        mask, scan = scratch(C), scratch(C)
        key, slot = [scratch(E1.cols), scratch(E2.cols)], [scratch(E1.cols), scratch(E2.cols)]
        rec = [scratch(E1.cols * 2).rearrange("p (c w) -> p c w", w=2),
               scratch(E2.cols * 2).rearrange("p (c w) -> p c w", w=2)]
        raw_i = scratch(C).bitcast(I32)
        raw_j = scratch(C).bitcast(I32)
        empty = list2
        zrow = sb1("zrow", [1, 2 * (P + 1)])
        counts = sb1("counts", [P, B])
        cnt_i = sb1("cnt_i", [P, B], I32)
        ntile = sb1("ntile", [P, B])
        tend = sb1("tend", [P, B])
        off = sb1("off", [P, B])
        bsum = sb1("bsum", [P, B])
        tend_c = sb1("tend_c", [P, 1])
        recring = sb1("recring", [P, 2, 16, 2])
        slotring = sb1("slotring", [P, 2, 16], I32)

        W1s = sb1("W1s", [P, 2, HID])
        W2s = sb1("W2s", [P, 1])
        b1s = sb1("b1s", [P, 1])
        b2s = sb1("b2s", [1, 1])
        wqs = sb1("wqs", [P, 2, D])
        wks = sb1("wks", [P, 2, D])
        wvs = sb1("wvs", [P, 2, D])
        wos = sb1("wos", [P, 2, D])
        bqs = sb1("bqs", [P, 2])
        rows = sb1("rows", [1, 3, D])
        xn = sb1("xn", [P, D])
        xt = sb1("xt", [P, 2, P])
        hT = sb1("hT", [P, P])
        kmin = sb1("kmin", [P, D])
        kexp = sb1("kexp", [P, D])
        kf = sb1("kf", [P, D])
        vt = sb1("vt", [P, 2, P + 1])
        wexp = sb1("wexp", [P, 2])
        yt = sb1("yt", [P, YW])
        kv = sb1("kv", [P, 2, P])
        ks = sb1("ks", [P, 2, P])
        qmin = sb1("qmin", [P, 2, P])
        qexp = sb1("qexp", [P, 2, P])
        qf = sb1("qf", [P, 2, P])
        oT = sb1("oT", [P, 2, P])

        p_tp = ps1("p_tp", [P, 512])
        p_h = ps1("p_h", [P, 512])
        p_k = ps1("p_k", [P, 512])
        p_v = ps1("p_v", [P, 512])
        p_z = ps1("p_z", [P, 512])
        p_kv = ps1("p_kv", [P, 512])
        p_cnt = ps1("p_cnt", [P, 512])
        p_blk = ps1("p_blk", [P, 512])
        kv_acc = p_kv[:, 0:2 * (P + 1)].rearrange("p (c w) -> p c w", c=2)

        loaded, made, x_in, res_zero = sem1("loaded"), sem1("made"), sem1("x_in"), sem1("res_zero")
        ids_in = [sem1("ids1_in"), sem1("ids2_in")]
        dve_done = sem1("dve_done")
        ids_free = sem1("ids_free")
        iota_made = sem1("iota_made")
        counts_ready, sums_ready = sem1("counts_ready"), sem1("sums_ready")
        ge_ready, blk_ready, blk_taken = sem1("ge_ready"), sem1("blk_ready"), sem1("blk_taken")
        slots_ready, empty_made, empty_in = sem1("slots_ready"), sem1("empty_made"), sem1("empty_in")
        ring_full = [sem1("ring0_full"), sem1("ring1_full")]
        half_out = [sem1("half0_out"), sem1("half1_out")]
        a_xn, a_tp, a_xt, a_mm, a_h, a_z = (sem1(n) for n in ("a_xn", "a_tp", "a_xt", "a_mm", "a_h", "a_z"))
        a_min, a_exp, a_kv, a_wexp, a_y, a_kvdone = (sem1(n) for n in ("a_min", "a_exp", "a_kv", "a_wexp", "a_y", "a_kvdone"))
        y_out, kv_zero, kv_all, kv_ready = sem1("y_out"), sem1("kv_zero"), sem1("kv_all"), sem1("kv_ready")
        var_ready, sd_ready = sem1("var_ready"), sem1("sd_ready")
        q_mm, q_min, q_exp, q_feat, q_att, q_o, q_mix, q_done = (
            sem1(n) for n in ("q_mm", "q_min", "q_exp", "q_feat", "q_att", "q_o", "q_mix", "q_done"))
        lists_in = sem1("lists_in")

        block = c1.enter_context(nc.Block())
        EDGES = ((E1, src.rearrange("(p c) -> p c", p=E1.parts), dst.rearrange("(p c) -> p c", p=E1.parts), True),
                 (E2, edge_index[0].rearrange("(p c) -> p c", p=P), edge_index[1].rearrange("(p c) -> p c", p=P), False))

        @block.sync
        def _(sp):
            sp.dma_start(raw_i[0:E1.parts, 0:E1.cols], EDGES[0][1]).then_inc(ids_in[0], 16)
            sp.dma_start(raw_j[0:E1.parts, 0:E1.cols], EDGES[0][2]).then_inc(ids_in[0], 16)
            sp.dma_start(res[:, 0:FULL, :], x[0:FULL * P].rearrange("(b p) d -> p b d", p=P)).then_inc(x_in, 16)
            sp.wait_ge(res_zero, 1)
            sp.dma_start(res[0:LAST, FULL, :], x[FULL * P:]).then_inc(x_in, 16)
            for w, a in ((W1s, gW1), (wqs, wq), (wks, wk), (wvs, wv), (wos, wo)):
                sp.dma_start(w[:], a.rearrange("(c p) n -> p c n", p=P)).then_inc(loaded, 16)
            sp.dma_start(W2s[:], gW2).then_inc(loaded, 16)
            sp.dma_start(b1s[:], gb1.rearrange("(p o) -> p o", o=1)).then_inc(loaded, 16)
            sp.dma_start(b2s[:], gb2.rearrange("(p o) -> p o", o=1)).then_inc(loaded, 16)
            for c in range(2):
                sp.dma_start(bqs[:, c:c + 1], bq[c * P:(c + 1) * P].rearrange("(p o) -> p o", o=1)).then_inc(loaded, 16)
            for n, a in enumerate((bk, bv, bo)):
                sp.dma_start(rows[:, n, :], a.rearrange("(o d) -> o d", o=1)).then_inc(loaded, 16)
            sp.wait_ge(empty_made, 2)
            sp.dma_start(list1_dram.rearrange("(p t) w -> p t w", p=P), empty[:, 0:T1, :]).then_inc(empty_in, 16)
            sp.dma_start(list2_dram.rearrange("(p t) w -> p t w", p=P), empty[:, 0:T2, :]).then_inc(empty_in, 16)
            sp.wait_ge(ids_free, 1)
            sp.dma_start(raw_i[:, 0:E2.cols], EDGES[1][1]).then_inc(ids_in[1], 16)
            sp.dma_start(raw_j[:, 0:E2.cols], EDGES[1][2]).then_inc(ids_in[1], 16)
            halves = 0
            for g, (E, _, _, _) in enumerate(EDGES):
                U, q = E.unroll, E.parts
                sp.wait_ge(slots_ready, g + 1)
                with sp.Fori(0, E.cols // (2 * U)) as i:
                    for half in range(2):
                        sp.wait_ge(half_out[half], i * (16 * U) + (0 if g == 0 else 8 * E1.cols))
                        c0 = i * (2 * U) + half * U
                        sp.dma_start(recring[0:q, half, 0:U, :], rec[g][0:q, bass.ds(c0, U), :]).then_inc(ring_full[half], 16)
                        sp.dma_start(slotring[0:q, half, 0:U],
                                     key[g].bitcast(I32)[0:q, bass.ds(c0, U)]).then_inc(ring_full[half], 16)
            sp.wait_ge(half_out[0], 16 * (E1.cols + E2.cols) // 2)
            sp.wait_ge(half_out[1], 16 * (E1.cols + E2.cols) // 2)
            sp.dma_start(list1[:], list1_dram.rearrange("(p t) w -> p t w", p=P)).then_inc(lists_in, 16)
            sp.dma_start(list2[:], list2_dram.rearrange("(p t) w -> p t w", p=P)).then_inc(lists_in, 16)
            sp.wait_ge(lists_in, 32)

        @block.gpsimd
        def _(pool):
            pool.memset(zero1[:], 0.0).then_inc(made, 1)
            pool.memset(res[:, FULL, :], 0.0).then_inc(res_zero, 1)
            pool.iota(lane[:], [[1, P]], base=0, channel_multiplier=0,
                      allow_small_or_imprecise_dtypes=True).then_inc(iota_made, 1)
            pool.memset(empty[:, :, 0], 0.0).then_inc(empty_made, 1)
            pool.memset(empty[:, :, 1], -1.0).then_inc(empty_made, 1)
            pool.memset(ones[:], 1.0).then_inc(made, 1)
            pool.memset(ident[:], 0.0).then_inc(made, 1)
            pool.memset(valid[:], 1.0).then_inc(made, 1)
            pool.memset(zrow[:], 0.0).then_inc(made, 1)
            pool.wait_ge(made, 5)
            pool.affine_select(out=ident[:], in_=ident[:], compare_op=ALU.not_equal, fill=1.0, base=0,
                               pattern=[[-1, P]], channel_multiplier=1).then_inc(made, 1)
            pool.affine_select(out=before[:], in_=ones[:], compare_op=ALU.is_gt, fill=0.0, base=0,
                               pattern=[[1, P]], channel_multiplier=-1).then_inc(made, 1)
            pool.affine_select(out=valid[:], in_=valid[:], compare_op=ALU.is_ge, fill=0.0, base=N - 1,
                               pattern=[[-P, B]], channel_multiplier=-1).then_inc(made, 1)
            halves = 0
            pool.wait_ge(empty_in, 32)
            for g, (E, _, _, _) in enumerate(EDGES):
                target = (list1_dram, list2_dram)[g]
                U, T, n_loop = E.unroll, E.tiles, E.cols // (2 * E.unroll)
                last_row = pool.to_reg(P * T - 1)
                with pool.Fori(0, n_loop) as i:
                    for half in range(2):
                        pool.wait_ge(ring_full[half], halves + i * 32 + 32)
                        pool.wait_ge(turned, turns[0] + 2 * i + half)
                        pool.tensor_tensor(turn[:], zero1[:], zero1[:], ALU.add).then_inc(turned, 1)
                        for u in range(U):
                            pool.indirect_dma_start(
                                target, bass.IndirectOffsetOnAxis(ap=slotring[0:E.parts, half, u:u + 1], axis=0),
                                recring[0:E.parts, half, u, :], None,
                                bounds_check=last_row, oob_is_err=False).then_inc(half_out[half], 16)
                halves += 32 * n_loop
                turns[0] += 2 * n_loop

        @block.vector
        def _(dve):
            s = Steps(dve, dve_done)

            def rank(g):
                E, _, _, swapped = EDGES[g]
                q, Cn, T = E.parts, E.cols, E.tiles
                k, r, e = key[g][0:q], slot[g][0:q], rec[g]
                m, sc = mask[0:q, 0:Cn], scan[0:q, 0:Cn]
                source, target = (raw_j, raw_i) if swapped else (raw_i, raw_j)
                source, target = source[0:q, 0:Cn], target[0:q, 0:Cn]
                dve.wait_ge(ids_in[g], 32)
                s.step(dve.memset(counts[:], 0.0))
                s.did(dve.tensor_scalar(sc.bitcast(I32), target, 7, None, ALU.logical_shift_right))
                s.did(dve.tensor_scalar(m.bitcast(I32), target, P - 1, None, ALU.bitwise_and))
                s.did(dve.tensor_scalar(e[0:q, :, 0], source, float(N - 1), None, ALU.min))
                s.settle()
                s.did(dve.tensor_copy(k, sc.bitcast(I32)))
                s.step(dve.tensor_copy(e[0:q, :, 1], m.bitcast(I32)))
                s.did(dve.tensor_scalar(r, k, float(B), FAR, ALU.is_ge, ALU.mult))
                if g == 0:
                    dve.nop().then_inc(ids_free, 1)
                s.settle()
                start = s.n
                with dve.Fori(0, B) as b:
                    l = Steps(dve, dve_done, start + b * 5)
                    l.step(dve.tensor_scalar(m, k, lane[0:q, bass.ds(b, 1)], None, ALU.is_equal))
                    l.step(dve.tensor_tensor_scan(sc, m, m, 0.0, ALU.add, ALU.max))
                    l.step(dve.tensor_copy(counts[0:q, bass.ds(b, 1)], sc[:, Cn - 1:Cn]))
                    l.step(dve.tensor_tensor(sc, sc, m, ALU.mult))
                    l.step(dve.tensor_tensor(r, r, sc, ALU.add))
                s.n = start + B * 5
                dve.nop().then_inc(counts_ready, 1)
                dve.wait_ge(sums_ready, g + 1)
                s.step(dve.tensor_copy(cnt_i[:], p_cnt[:, B:2 * B]))
                s.step(dve.tensor_scalar(cnt_i[:], cnt_i[:], float(P - 1), None, ALU.add))
                s.step(dve.tensor_scalar(cnt_i[:], cnt_i[:], 7, None, ALU.logical_shift_right))
                s.step(dve.tensor_copy(ntile[:], cnt_i[:]))
                s.step(dve.tensor_tensor_scan(tend[:], ntile[:], ntile[:], 0.0, ALU.add, ALU.max))
                s.step(dve.tensor_tensor(off[:], tend[:], ntile[:], ALU.subtract))
                s.step(dve.tensor_scalar(off[:], off[:], float(P), -1.0, ALU.mult, ALU.add))
                s.step(dve.tensor_tensor(off[:], off[:], p_cnt[:, 0:B], ALU.add))
                s.step(dve.tensor_tensor(bsum[0:B, :], tend[0:B, :], ident[0:B, 0:B], ALU.mult))
                s.step(dve.tensor_reduce(tend_c[0:B, :], bsum[0:B, :], AX.X, ALU.add))
                n_part = -(-T // 512)
                for part in range(n_part):
                    w = min(512, T - 512 * part)
                    for a in range(0, w, P):
                        z = min(P, w - a)
                        s.did(dve.tensor_scalar(mask[0:B, a:a + z], lane[0:B, 0:z], float(512 * part + a),
                                                tend_c[0:B, 0:1], ALU.add, ALU.is_ge))
                    s.settle()
                    dve.nop().then_inc(ge_ready, 1)
                    dve.wait_ge(blk_ready, blk_done[0] + 1)
                    blk_done[0] += 1
                    s.step(dve.tensor_scalar((blk1, blk2)[g][0:1, 512 * part:512 * part + w], p_blk[0:1, 0:w],
                                             float(B - 1), None, ALU.min))
                start = s.n
                with dve.Fori(0, B) as b:
                    l = Steps(dve, dve_done, start + b * 2)
                    l.step(dve.tensor_scalar(m, k, lane[0:q, bass.ds(b, 1)], None, ALU.is_equal))
                    l.step(dve.scalar_tensor_tensor(out=r, in0=m, scalar=off[0:q, bass.ds(b, 1)], in1=r,
                                                    op0=ALU.mult, op1=ALU.add))
                s.n = start + B * 2
                s.step(dve.tensor_copy(sc.bitcast(I32), r))
                s.did(dve.tensor_scalar(m.bitcast(I32), sc.bitcast(I32), P - 1, None, ALU.bitwise_and))
                s.step(dve.tensor_scalar(k.bitcast(I32), sc.bitcast(I32), 7, None, ALU.logical_shift_right))
                s.did(dve.tensor_copy(r, m.bitcast(I32)))
                s.step(dve.tensor_copy(sc, k.bitcast(I32)))
                s.step(dve.scalar_tensor_tensor(out=r, in0=r, scalar=float(T), in1=sc, op0=ALU.mult, op1=ALU.add))
                s.step(dve.tensor_scalar(m, sc, float(T), FAR, ALU.is_ge, ALU.mult))
                s.step(dve.tensor_tensor(r, r, m, ALU.add))
                s.step(dve.tensor_copy(k.bitcast(I32), r))
                dve.nop().then_inc(slots_ready, 1)

            blk_done = [0]
            dve.wait_ge(iota_made, 1)
            dve.wait_ge(made, 8)
            rank(0)

            s.step(dve.memset(epsc[:], LN_EPS))
            dve.wait_ge(x_in, 32)
            start = s.n
            with dve.Fori(0, B) as b:
                dve.bn_stats(bst[:, bass.ds(b, 1), :].rearrange("p o w -> p (o w)"),
                             res[:, bass.ds(b, 1), :].rearrange("p o d -> p (o d)")).then_inc(dve_done, 1)
            s.n = start + B
            s.settle()
            for b in range(B):
                s.did(dve.bn_aggr(mean[:, b, :], bst[:, b, :]))
            s.settle()
            dve.nop().then_inc(var_ready, 1)
            dve.wait_ge(sd_ready, 1)
            s.step(dve.reciprocal(rstd[:], rstd[:]))

            start = s.n
            with dve.Fori(0, B) as b:
                l = Steps(dve, dve_done, start + 5 * b)
                dve.wait_ge(y_out, 16 * b)
                dve.tensor_scalar(xn[:], res[:, bass.ds(b, 1), :].rearrange("p o d -> p (o d)"),
                                  mean[:, bass.ds(b, 1), 0:1].rearrange("p o w -> p (o w)"),
                                  rstd[:, bass.ds(b, 1)], ALU.subtract, ALU.mult).then_inc(a_xn, 1)
                dve.wait_ge(a_mm, b + 1)
                dve.tensor_scalar(kmin[:], p_k[:, 0:D], 0.0, None, ALU.min).then_inc(a_min, 1)
                dve.wait_ge(a_kvdone, b)
                for c in range(2):
                    l.did(dve.tensor_scalar(vt[:, c, 0:P], p_v[:, c * P:(c + 1) * P], valid[:, bass.ds(b, 1)],
                                            None, ALU.mult))
                    dve.tensor_copy(vt[:, c, P:P + 1], valid[:, bass.ds(b, 1)]).then_inc(kv_zero, 1)
                dve.wait_ge(a_exp, b + 1)
                l.did(dve.scalar_tensor_tensor(out=kf[:], in0=p_k[:, 0:D], scalar=0.0, in1=kexp[:],
                                               op0=ALU.max, op1=ALU.add))
                l.settle()
                dve.nop().then_inc(a_kv, 1)
                dve.wait_ge(a_wexp, b + 1)
                l.step(dve.tensor_scalar(wexp[:, 1:2], wexp[:, 0:1], 1.0, None, ALU.add))
                l.step(dve.reciprocal(yt[:, D:YW], wexp[:, 1:2]))
                dve.tensor_scalar(yt[:, 0:D], xn[:], yt[:, D:YW], None, ALU.mult).then_inc(a_y, 1)
            s.n = start + 5 * B

            rank(1)

            dve.wait_ge(kv_all, 1)
            s.did(dve.memset(kv[:], 0.0))
            s.step(dve.memset(ks[:], 0.0))
            for c in range(2):
                for h in range(P // MD):
                    d = slice(h * MD, (h + 1) * MD)
                    s.did(dve.tensor_copy(kv[d, c, d], kv_acc[d, c, d]))
                    s.did(dve.tensor_scalar(ks[d, c, d], ones[d, d], kv_acc[d, c, P:P + 1], None, ALU.mult))
            s.settle()
            dve.nop().then_inc(kv_ready, 1)
            start = s.n
            with dve.Fori(0, B) as b:
                l = Steps(dve, dve_done, start + 5 * b)
                dve.wait_ge(q_mm, b + 1)
                for c in range(2):
                    l.did(dve.tensor_scalar(qmin[:, c, :], p_tp[:, c * P:(c + 1) * P], bqs[:, c:c + 1], 0.0,
                                            ALU.add, ALU.min))
                l.settle()
                dve.nop().then_inc(q_min, 1)
                for c in range(2):
                    l.did(dve.tensor_scalar(qf[:, c, :], p_tp[:, c * P:(c + 1) * P], bqs[:, c:c + 1], 0.0,
                                            ALU.add, ALU.max))
                l.settle()
                dve.wait_ge(q_exp, b + 1)
                dve.tensor_tensor(qf[:], qf[:], qexp[:], ALU.add).then_inc(q_feat, 1)
                dve.wait_ge(q_att, b + 1)
                l2 = p_k[:, 0:2 * P].rearrange("p (c n) -> p c n", c=2)
                l3 = p_v[:, 0:2 * P].rearrange("p (c n) -> p c n", c=2)
                l.step(dve.tensor_scalar(oT[:], l3, 1e-6, None, ALU.add))
                dve.reciprocal(oT[:], oT[:]).then_inc(q_o, 1)
                dve.wait_ge(q_o, 2 * b + 1)
                dve.tensor_tensor(oT[:], oT[:], l2, ALU.mult).then_inc(q_o, 1)
                dve.wait_ge(q_mix, b + 1)
                r = res[:, bass.ds(b, 1), :].rearrange("p o d -> p (o d)")
                dve.tensor_tensor(r, r, p_h[:, 0:D], ALU.add).then_inc(q_done, 1)
            s.n = start + 5 * B

        @block.scalar
        def _(act):
            act.wait_ge(var_ready, 1)
            nc.scalar.activation(rstd[:], mean[:, :, 1], ACT.Sqrt, bias=epsc[:, 0:1]).then_inc(sd_ready, 1)
            act.wait_ge(loaded, 16 * 13)
            with act.Fori(0, B) as b:
                act.wait_ge(a_tp, b + 1)
                t = p_tp[:, 0:D].rearrange("p (c n) -> p c n", c=2)
                nc.scalar.copy(xt[:], t).then_inc(a_xt, 1)
                nc.scalar.copy(xnT[:, :, bass.ds(b * P, P)], t).then_inc(a_xt, 1)
                act.wait_ge(a_mm, b + 1)
                nc.scalar.activation(hT[:], p_h[:, 0:P], ACT.Relu, bias=b1s[:, 0:1]).then_inc(a_h, 1)
                act.wait_ge(a_min, b + 1)
                nc.scalar.activation(kexp[:], kmin[:], ACT.Exp).then_inc(a_exp, 1)
                act.wait_ge(a_z, b + 1)
                nc.scalar.activation(wexp[:, 0:1], p_z[:, 0:1], ACT.Exp, scale=-1.0).then_inc(a_wexp, 1)
                act.wait_ge(a_y, b + 1)
                act.dma_start(y_dram[bass.ds(b * P, P), :], yt[:]).then_inc(y_out, 16)
            act.wait_ge(y_out, 16 * B)
            act.nop().then_inc(y_stored, 1)
            with act.Fori(0, B) as b:
                act.wait_ge(q_min, b + 1)
                nc.scalar.activation(qexp[:], qmin[:], ACT.Exp).then_inc(q_exp, 1)

        @block.tensor
        def _(pe):
            blk_n = [0]

            def sums(g):
                T = EDGES[g][0].tiles
                pe.wait_ge(counts_ready, g + 1)
                nc.tensor.matmul(p_cnt[:, 0:B], before[:], counts[:], start=True, stop=True)
                nc.tensor.matmul(p_cnt[:, B:2 * B], ones[:], counts[:], start=True, stop=True).then_inc(sums_ready, 1)
                for part in range(-(-T // 512)):
                    w = min(512, T - 512 * part)
                    blk_n[0] += 1
                    pe.wait_ge(ge_ready, blk_n[0])
                    nc.tensor.matmul(p_blk[0:1, 0:w], ones[0:B, 0:1], mask[0:B, 0:w], start=True,
                                     stop=True).then_inc(blk_ready, 1)

            sums(0)
            pe.wait_ge(loaded, 16 * 13)
            nc.tensor.matmul(kv_acc, zrow[:, 0:P], zrow[:], start=True, stop=False,
                             skip_group_check=True)
            with pe.Fori(0, B) as b:
                pe.wait_ge(a_xn, b + 1)
                pe.wait_ge(a_wexp, b)
                nc.tensor.transpose(p_tp[:, 0:P], xn[:, 0:P], ident[:])
                nc.tensor.transpose(p_tp[:, P:D], xn[:, P:D], ident[:]).then_inc(a_tp, 1)
                pe.wait_ge(a_xt, 2 * b + 1)
                for c in range(2):
                    nc.tensor.matmul(p_h[:, 0:P], W1s[:, c, :], xt[:, c, :], start=(c == 0), stop=(c == 1))
                for w, o, r in ((wks, p_k, 0), (wvs, p_v, 1)):
                    for c in range(2):
                        nc.tensor.matmul(o[:, 0:D], xt[:, c, :], w[:, c, :], start=(c == 0), stop=False)
                    last = nc.tensor.matmul(o[:, 0:D], ones[0:1, :], rows[0:1, r, :], start=False, stop=True)
                last.then_inc(a_mm, 1)
                pe.wait_ge(a_h, b + 1)
                nc.tensor.matmul(p_z[:, 0:1], hT[:], W2s[:], start=True, stop=False)
                nc.tensor.matmul(p_z[:, 0:1], ones[0:1, :], b2s[:], start=False, stop=True).then_inc(a_z, 1)
                pe.wait_ge(a_kv, b + 1)
                pe.wait_ge(kv_zero, 2 * b + 2)
                for c in range(2):
                    last = nc.tensor.matmul(kv_acc[:, c, :], kf[:, c * P:(c + 1) * P], vt[:, c, :],
                                            start=False, stop=False, skip_group_check=True)
                last.then_inc(a_kvdone, 1)
                pe.wait_ge(a_xt, 2 * b + 2)
            nc.tensor.matmul(kv_acc, zrow[:, 0:P], zrow[:], start=False, stop=True,
                             skip_group_check=True).then_inc(kv_all, 1)
            sums(1)
            pe.wait_ge(kv_ready, 1)
            with pe.Fori(0, B) as b:
                for m in range(2):
                    for c in range(2):
                        last = nc.tensor.matmul(p_tp[:, m * P:(m + 1) * P], wqs[:, c, m * P:(m + 1) * P],
                                                xnT[:, c, bass.ds(b * P, P)], start=(c == 0), stop=(c == 1))
                last.then_inc(q_mm, 1)
                pe.wait_ge(q_feat, b + 1)
                for m in range(2):
                    nc.tensor.matmul(p_k[:, m * P:(m + 1) * P], kv[:, m, :], qf[:, m, :], start=True, stop=True)
                    last = nc.tensor.matmul(p_v[:, m * P:(m + 1) * P], ks[:, m, :], qf[:, m, :], start=True, stop=True)
                last.then_inc(q_att, 1)
                pe.wait_ge(q_o, 2 * b + 2)
                pe.wait_ge(q_done, b)
                for c in range(2):
                    nc.tensor.matmul(p_h[:, 0:D], oT[:, c, :], wos[:, c, :], start=(c == 0), stop=False)
                nc.tensor.matmul(p_h[:, 0:D], ones[0:1, :], rows[0:1, 2, :], start=False, stop=True).then_inc(q_mix, 1)

    if stop_after == 1:
        debug(nc, locals())
        ctx.close()
        return

    with ExitStack() as c2:
        def sb2(name, shape, dt=F32):
            return c2.enter_context(nc.sbuf_tensor(name, shape, dt))

        def sem2(name):
            return c2.enter_context(nc.semaphore(name))

        idx = sb2("g_idx", [P, G], I32)
        rowsg = sb2("g_rows", [P, G, YW])
        hot = sb2("g_hot", [P, G, P])
        p_sum = [c2.enter_context(nc.psum_tensor(f"g_sum{j}", [P, 512], F32)) for j in range(G)]
        g_zero, g_idx = sem2("g_zero"), sem2("g_idx_ready")
        gath, free = [sem2("g_gath0"), sem2("g_gath1")], [sem2("g_free0"), sem2("g_free1")]
        g_hot, g_mm, g_sum = sem2("g_hot_ready"), sem2("g_mm"), [sem2("g_sum0"), sem2("g_sum1")]
        block = c2.enter_context(nc.Block())

        @block.scalar
        def _(act):
            with act.Fori(0, T1 // G) as i:
                for h in range(2):
                    act.wait_ge(gath[h], i * (16 * HG))
                    nc.scalar.copy(idx[:, h * HG:(h + 1) * HG],
                                   list1[:, bass.ds(i * G + h * HG, HG), 0]).then_inc(g_idx, 1)

        @block.gpsimd
        def _(pool):
            pool.wait_ge(y_stored, 1)
            with pool.Fori(0, T1 // G) as i:
                for h in range(2):
                    pool.wait_ge(g_idx, 2 * i + h + 1)
                    pool.wait_ge(free[h], i)
                    pool.wait_ge(turned, turns[0] + 2 * i + h)
                    pool.tensor_tensor(turn[:], zero1[:], zero1[:], ALU.add).then_inc(turned, 1)
                    for j in range(h * HG, (h + 1) * HG):
                        pool.indirect_dma_start(rowsg[:, j, :], None, y_dram,
                                                bass.IndirectOffsetOnAxis(ap=idx[:, j:j + 1], axis=0)
                                                ).then_inc(gath[h], 16)
            turns[0] += 2 * (T1 // G)

        @block.tensor
        def _(pe):
            with pe.Fori(0, T1 // G) as i:
                for h in range(2):
                    pe.wait_ge(gath[h], i * (16 * HG) + 16 * HG)
                    pe.wait_ge(g_hot, i * G + (h + 1) * HG)
                    pe.wait_ge(g_sum[h], i * HG)
                    for j in range(h * HG, (h + 1) * HG):
                        mm = nc.tensor.matmul(p_sum[j][:, 0:YW], hot[:, j, :], rowsg[:, j, :], start=True, stop=True)
                        mm.then_inc(g_mm, 1)
                    pe.wait_ge(g_mm, i * G + (h + 1) * HG)
                    pe.nop().then_inc(free[h], 1)

        @block.vector
        def _(dve):
            dve.memset(acc, 0.0).then_inc(g_zero, 1)
            dve.wait_ge(g_zero, 1)
            with dve.Fori(0, T1 // G) as i:
                for h in range(2):
                    dve.wait_ge(free[h], i)
                    for j in range(h * HG, (h + 1) * HG):
                        dve.tensor_scalar(hot[:, j, :], lane[:], list1[:, bass.ds(i * G + j, 1), 1], None,
                                          ALU.is_equal).then_inc(g_hot, 1)
                    for j in range(h * HG, (h + 1) * HG):
                        b = dve.value_load(blk1[0:1, bass.ds(i * G + j, 1)], min_val=0, max_val=B - 1)
                        a = acc[:, bass.ds(b, 1), :].rearrange("p o w -> p (o w)")
                        dve.wait_ge(g_mm, i * G + j + 1)
                        dve.wait_ge(g_sum[0], i * HG + (j if h == 0 else HG))
                        dve.wait_ge(g_sum[1], i * HG + (0 if h == 0 else j - HG))
                        dve.tensor_tensor(a, a, p_sum[j][:, 0:YW], ALU.add).then_inc(g_sum[h], 1)

    node = sb("node", [P, B, RW + HEADS])
    late = sb("late", [P, B, 2 * HEADS])
    vmax = sb("vmax", [P, B, HEADS])
    asum = sb("asum", [P, B, HEADS + HE])
    gate = sb("gate", [P, B, EXPERTS])
    A_S, H0, A_D = HEADS, 2 * HEADS, 2 * HEADS + HE
    with ExitStack() as c3:
        def sb3(name, shape, dt=F32):
            return c3.enter_context(nc.sbuf_tensor(name, shape, dt))

        def sem3(name):
            return c3.enter_context(nc.semaphore(name))

        Wg = sb3("Wg", [P, 2, HE])
        att = sb3("att", [P, 2, HE])
        den = sb3("den", [P, B])
        xn = sb3("x_xn", [P, D])
        xt = sb3("x_xt", [P, 2, P])
        prod = sb3("x_prod", [P, 2, HE])
        low = sb3("low", [P, HEADS])
        neg = sb3("neg", [P, HEADS])
        p_t = c3.enter_context(nc.psum_tensor("x_pt", [P, 512], F32))
        p_g = c3.enter_context(nc.psum_tensor("x_pg", [P, 512], F32))
        x_load, x_done, x_var, x_sd = sem3("x_load"), sem3("x_done"), sem3("x_var"), sem3("x_sd")
        x_xn, x_tp, x_xt, x_h = sem3("x_xn_ready"), sem3("x_tp"), sem3("x_xt_ready"), sem3("x_h")
        x_low, x_neg, x_node, x_out = sem3("x_low"), sem3("x_neg"), sem3("x_node"), sem3("x_out")
        block = c3.enter_context(nc.Block())

        @block.sync
        def _(sp):
            sp.dma_start(Wg[:], W_gat.rearrange("(c p) n -> p c n", p=P)).then_inc(x_load, 16)
            for n, a in enumerate((att_src, att_dst)):
                sp.dma_start(att[:, n, :], a.rearrange("h e -> (h e)").partition_broadcast(P)).then_inc(x_load, 16)
            sp.wait_ge(x_node, 1)
            sp.dma_start(node_dram.rearrange("(b p) w -> p b w", p=P), node[:, :, 0:RW]).then_inc(x_out, 16)
            sp.wait_ge(x_out, 16)
            sp.nop().then_inc(node_stored, 1)

        @block.vector
        def _(dve):
            s = Steps(dve, x_done)
            s.step(dve.tensor_scalar(den[:], acc[:, :, D], 1e-12, None, ALU.max))
            s.step(dve.reciprocal(den[:], den[:]))
            start = s.n
            with dve.Fori(0, B) as b:
                r = res[:, bass.ds(b, 1), :].rearrange("p o d -> p (o d)")
                a = acc[:, bass.ds(b, 1), 0:D].rearrange("p o d -> p (o d)")
                dve.scalar_tensor_tensor(out=r, in0=a, scalar=den[:, bass.ds(b, 1)], in1=r,
                                         op0=ALU.mult, op1=ALU.add).then_inc(x_done, 1)
            s.n = start + B
            s.settle()
            with dve.Fori(0, B) as b:
                dve.bn_stats(bst[:, bass.ds(b, 1), :].rearrange("p o w -> p (o w)"),
                             res[:, bass.ds(b, 1), :].rearrange("p o d -> p (o d)")).then_inc(x_done, 1)
            s.n = start + 2 * B
            s.settle()
            for b in range(B):
                s.did(dve.bn_aggr(mean[:, b, :], bst[:, b, :]))
            s.settle()
            dve.nop().then_inc(x_var, 1)
            dve.wait_ge(x_sd, 1)
            s.step(dve.reciprocal(rstd[:], rstd[:]))
            dve.wait_ge(x_load, 48)
            start = s.n
            with dve.Fori(0, B) as b:
                l = Steps(dve, x_done, start + 4 * b)
                dve.tensor_scalar(xn[:], res[:, bass.ds(b, 1), :].rearrange("p o d -> p (o d)"),
                                  mean[:, bass.ds(b, 1), 0:1].rearrange("p o w -> p (o w)"),
                                  rstd[:, bass.ds(b, 1)], ALU.subtract, ALU.mult).then_inc(x_xn, 1)
                dve.wait_ge(x_h, b + 1)
                hb = p_g[:, 0:HE]
                nb = node[:, bass.ds(b, 1), :].rearrange("p o w -> p (o w)")
                l.did(dve.tensor_copy(nb[:, H0:H0 + HE], hb))
                l.step(dve.tensor_tensor(prod[:], att[:], hb.unsqueeze(1).broadcast_to([P, 2, HE]), ALU.mult))
                for n, o in enumerate((A_S, A_D)):
                    l.did(dve.tensor_reduce(nb[:, o:o + HEADS], prod[:, n, :].rearrange("p (h e) -> p h e", h=HEADS),
                                            AX.X, ALU.add))
                l.settle()
            s.n = start + 4 * B
            s.step(dve.tensor_reduce(low[:], node[:, :, A_S:A_S + HEADS].rearrange("p b h -> p h b"), AX.X, ALU.min))
            s.step(dve.tensor_scalar(low[:], low[:], -1.0, None, ALU.mult))
            dve.nop().then_inc(x_low, 1)
            dve.wait_ge(x_neg, 1)
            ngb = neg[:].unsqueeze(1).broadcast_to([P, B, HEADS])
            s.did(dve.tensor_tensor(node[:, :, 0:HEADS], node[:, :, A_S:A_S + HEADS], ngb, ALU.add))
            s.did(dve.tensor_tensor(late[:, :, 0:HEADS], node[:, :, A_D:A_D + HEADS], ngb, ALU.subtract))
            s.settle()
            dve.nop().then_inc(x_node, 1)
            s.step(dve.tensor_copy(vmax[:], node[:, :, 0:HEADS]))

        @block.gpsimd
        def _(pool):
            pool.wait_ge(x_low, 1)
            pool.partition_all_reduce(neg[:], low[:], P, RED.max).then_inc(x_neg, 1)

        @block.scalar
        def _(act):
            act.wait_ge(x_var, 1)
            nc.scalar.activation(rstd[:], mean[:, :, 1], ACT.Sqrt, bias=epsc[:, 0:1]).then_inc(x_sd, 1)
            with act.Fori(0, B) as b:
                act.wait_ge(x_tp, b + 1)
                nc.scalar.copy(xt[:], p_t[:, 0:D].rearrange("p (c n) -> p c n", c=2)).then_inc(x_xt, 1)

        @block.tensor
        def _(pe):
            pe.wait_ge(x_load, 48)
            with pe.Fori(0, B) as b:
                pe.wait_ge(x_xn, b + 1)
                nc.tensor.transpose(p_t[:, 0:P], xn[:, 0:P], ident[:])
                nc.tensor.transpose(p_t[:, P:D], xn[:, P:D], ident[:]).then_inc(x_tp, 1)
                pe.wait_ge(x_xt, b + 1)
                nc.tensor.matmul(p_g[:, 0:HE], xt[:, 0, :], Wg[:, 0, :], start=True, stop=False)
                nc.tensor.matmul(p_g[:, 0:HE], xt[:, 1, :], Wg[:, 1, :], start=False, stop=True).then_inc(x_h, 1)

    if stop_after == 2:
        debug(nc, locals())
        ctx.close()
        return

    with ExitStack() as c4:
        def sb4(name, shape, dt=F32):
            return c4.enter_context(nc.sbuf_tensor(name, shape, dt))

        def sem4(name):
            return c4.enter_context(nc.semaphore(name))

        NB = 4
        idx = sb4("m_idx", [P, G], I32)
        rowsg = sb4("m_rows", [P, G, RW])
        hot = sb4("m_hot", [P, G, P])
        diag = sb4("m_diag", [P, NB, HEADS, P])
        best = sb4("m_best", [P, G, HEADS])
        p_max = [c4.enter_context(nc.psum_tensor(f"m_max{j}", [P, 512], F32)) for j in range(NB)]
        m_idx = sem4("m_idx_ready")
        gath, kept = [sem4("m_gath0"), sem4("m_gath1")], [sem4("m_kept0"), sem4("m_kept1")]
        m_hot, m_diag, m_mm, m_best, m_max = (sem4(n) for n in ("m_hot_ready", "m_diag_ready", "m_mm", "m_best_ready", "m_max_ready"))
        m_half = [sem4("m_half0"), sem4("m_half1")]
        block = c4.enter_context(nc.Block())

        @block.scalar
        def _(act):
            with act.Fori(0, T2 // G) as i:
                for h in range(2):
                    act.wait_ge(gath[h], i * (16 * HG))
                    nc.scalar.copy(idx[:, h * HG:(h + 1) * HG],
                                   list2[:, bass.ds(i * G + h * HG, HG), 0]).then_inc(m_idx, 1)
                for h in range(2):
                    act.wait_ge(gath[h], i * (16 * HG) + 16 * HG)
                    act.wait_ge(m_half[h], i + h)
                    for j in range(HG):
                        for k in range(HEADS):
                            nc.scalar.activation(diag[:, j, k, :], ident[:], ACT.Copy,
                                                 scale=rowsg[:, h * HG + j, k:k + 1]).then_inc(m_diag, 1)
                        if h == 0 and j == 0:
                            pass
                    nc.scalar.copy(gat[:, bass.ds(i * G + h * HG, HG), :],
                                   rowsg[:, h * HG:(h + 1) * HG, HEADS:RW]).then_inc(kept[h], 1)

        @block.gpsimd
        def _(pool):
            pool.wait_ge(node_stored, 1)
            with pool.Fori(0, T2 // G) as i:
                for h in range(2):
                    pool.wait_ge(m_idx, 2 * i + h + 1)
                    pool.wait_ge(kept[h], i)
                    pool.wait_ge(turned, turns[0] + 2 * i + h)
                    pool.tensor_tensor(turn[:], zero1[:], zero1[:], ALU.add).then_inc(turned, 1)
                    for j in range(h * HG, (h + 1) * HG):
                        pool.indirect_dma_start(rowsg[:, j, :], None, node_dram,
                                                bass.IndirectOffsetOnAxis(ap=idx[:, j:j + 1], axis=0)
                                                ).then_inc(gath[h], 16)
            turns[0] += 2 * (T2 // G)

        @block.tensor
        def _(pe):
            with pe.Fori(0, T2 // G) as i:
                for h in range(2):
                    pe.wait_ge(m_hot, i * G + (h + 1) * HG)
                    for j in range(HG):
                        pe.wait_ge(m_diag, (i * G + h * HG + j) * HEADS + HEADS)
                        pe.wait_ge(m_best, i * G + h * HG)
                        mm = nc.tensor.matmul(p_max[j][:], hot[:, h * HG + j, :],
                                              diag[:, j, :, :].rearrange("p h n -> p (h n)"), start=True, stop=True)
                        mm.then_inc(m_mm, 1)
                    pe.wait_ge(m_mm, i * G + (h + 1) * HG)
                    pe.nop().then_inc(m_half[1 - h], 1)

        @block.vector
        def _(dve):
            with dve.Fori(0, T2 // G) as i:
                for h in range(2):
                    dve.wait_ge(m_mm, i * G + h * HG)
                    for j in range(h * HG, (h + 1) * HG):
                        dve.tensor_scalar(hot[:, j, :], lane[:], list2[:, bass.ds(i * G + j, 1), 1], None,
                                          ALU.is_equal).then_inc(m_hot, 1)
                    for j in range(h * HG, (h + 1) * HG):
                        b = dve.value_load(blk2[0:1, bass.ds(i * G + j, 1)], min_val=0, max_val=B - 1)
                        v = vmax[:, bass.ds(b, 1), :].rearrange("p o w -> p (o w)")
                        dve.wait_ge(m_mm, i * G + j + 1)
                        dve.tensor_reduce(best[:, j, :], p_max[j % HG][:].rearrange("p (h n) -> p h n", h=HEADS),
                                          AX.X, ALU.max).then_inc(m_best, 1)
                        dve.wait_ge(m_best, i * G + j + 1)
                        dve.wait_ge(m_max, i * G + j)
                        dve.tensor_tensor(v, v, best[:, j, :], ALU.max).then_inc(m_max, 1)

    GS = 2 * G
    assert T2 % GS == 0
    with ExitStack() as c5:
        def sb5(name, shape, dt=F32):
            return c5.enter_context(nc.sbuf_tensor(name, shape, dt))

        def sem5(name):
            return c5.enter_context(nc.semaphore(name))

        hot = sb5("s_hot", [P, GS, P])
        hotT = sb5("s_hotT", [P, GS, P])
        z = sb5("s_z", [P, GS, HEADS])
        val = sb5("s_val", [P, GS, HEADS + HE])
        self_z = sb5("self_z", [P, B, HEADS])
        agg = hotT[:].rearrange("p j n -> p (j n)")[:, 0:B * HE].rearrange("p (b w) -> p b w", w=HE)
        sq = hot[:].rearrange("p j n -> p (j n)")[:, 0:B * HE].rearrange("p (b w) -> p b w", w=HE)
        mu = sb5("mu", [P, B])
        var = sb5("var", [P, B])
        sc = sb5("sc", [P, B, EXPERTS])
        less = sb5("less", [P, B])
        rank_ = sb5("rank_", [P, B, EXPERTS])
        top = sb5("top", [P, B])
        rowc = sb5("rowc", [P, 3, HE])
        p_T = [c5.enter_context(nc.psum_tensor(f"s_T{j}", [P, 512], F32)) for j in range(4)]
        p_e = [c5.enter_context(nc.psum_tensor(f"s_e{j}", [P, 512], F32)) for j in range(2)]
        p_s = [c5.enter_context(nc.psum_tensor(f"s_s{j}", [P, 512], F32)) for j in range(2)]
        s_step, s_hot, s_T, s_hotT, s_e, s_zr, s_exp, s_val, s_mm, s_sum, s_m, s_ld, s_a, s_b = (
            sem5(n) for n in ("s_step", "s_hot_ready", "s_T_ready", "s_hotT_ready", "s_e_ready", "s_z_ready", "s_exp",
                              "s_val_ready", "s_mm", "s_sum", "s_m", "s_ld", "s_a", "s_b"))
        s_v4 = sem5("s_v4")
        block = c5.enter_context(nc.Block())
        K = HEADS + HE

        @block.sync
        def _(sp):
            for n, a in enumerate((b_gat, ln_gamma, ln_beta)):
                sp.dma_start(rowc[:, n, :], a.partition_broadcast(P)).then_inc(s_ld, 16)

        @block.tensor
        def _(pe):
            pe.wait_ge(s_m, 1)
            with pe.Fori(0, T2 // GS) as i:
                for h in range(2):
                    for q in range(2):
                        pe.wait_ge(s_hot, (i * 2 + h) * G + (q + 1) * 4)
                        if True:
                            pe.wait_ge(s_hotT, i * 4)
                        for j in range(4):
                            mm = nc.tensor.transpose(p_T[2 * h + q][:, j * P:(j + 1) * P],
                                                     hot[:, h * G + q * 4 + j, :], ident[:])
                        mm.then_inc(s_T, 1)
                for h in range(2):
                    pe.wait_ge(s_zr, i * 2 + 0)
                    pe.wait_ge(s_hotT, i * 4 + 2 * h + 2)
                    for j in range(G):
                        b = pe.value_load(blk2[0:1, bass.ds(i * GS + h * G + j, 1)], min_val=0, max_val=B - 1)
                        mm = nc.tensor.matmul(p_e[h][:, j * 8:(j + 1) * 8], hotT[:, h * G + j, :],
                                              late[:, bass.ds(b, 1), :].rearrange("p o w -> p (o w)"),
                                              start=True, stop=True)
                    mm.then_inc(s_e, 1)
                for h in range(2):
                    pe.wait_ge(s_val, i * 2 + h + 1)
                    pe.wait_ge(s_sum, i * GS)
                    for j in range(G):
                        mm = nc.tensor.matmul(p_s[h][:, j * K:(j + 1) * K], hot[:, h * G + j, :], val[:, h * G + j, :],
                                              start=True, stop=True)
                    mm.then_inc(s_mm, 1)

        @block.scalar
        def _(act):
            act.wait_ge(s_a, 1)
            nc.scalar.activation(asum[:, :, 0:HEADS], self_z[:], ACT.Exp).then_inc(s_b, 1)
            with act.Fori(0, T2 // GS) as i:
                for h in range(2):
                    for q in range(2):
                        act.wait_ge(s_T, i * 4 + 2 * h + q + 1)
                        act.wait_ge(s_e, i * 2)
                        a = h * G + q * 4
                        nc.scalar.copy(hotT[:, a:a + 4, :].rearrange("p j n -> p (j n)"),
                                       p_T[2 * h + q][:]).then_inc(s_hotT, 1)
                for h in range(2):
                    act.wait_ge(s_zr, i * 2 + h + 1)
                    act.wait_ge(s_mm, i * 2)
                    nc.scalar.activation(val[:, h * G:(h + 1) * G, 0:HEADS], z[:, h * G:(h + 1) * G, :],
                                         ACT.Exp).then_inc(s_exp, 1)
            act.wait_ge(s_a, 2)
            nc.scalar.activation(var[:], var[:], ACT.Sqrt, bias=epsc[:, 0:1]).then_inc(s_b, 1)
            act.wait_ge(s_a, 3)
            nc.scalar.activation(gate[:], sc[:], ACT.Exp).then_inc(s_b, 1)

        @block.vector
        def _(dve):
            s = Steps(dve, s_step)
            mx = late[:, :, HEADS:2 * HEADS]
            ad = late[:, :, 0:HEADS]
            s.step(dve.tensor_tensor(mx, vmax[:], ad, ALU.add))
            s.step(dve.scalar_tensor_tensor(out=mx, in0=mx, scalar=0.2, in1=mx, op0=ALU.mult, op1=ALU.max))
            dve.nop().then_inc(s_m, 1)
            s.step(dve.tensor_tensor(self_z[:], node[:, :, A_S:A_S + HEADS], node[:, :, A_D:A_D + HEADS], ALU.add))
            s.step(dve.scalar_tensor_tensor(out=self_z[:], in0=self_z[:], scalar=0.2, in1=self_z[:],
                                            op0=ALU.mult, op1=ALU.max))
            s.step(dve.tensor_tensor(self_z[:], self_z[:], mx, ALU.subtract))
            s.step(dve.tensor_scalar(self_z[:], self_z[:], 0.0, None, ALU.min))
            dve.nop().then_inc(s_a, 1)
            dve.wait_ge(s_b, 1)
            for k in range(HEADS):
                e = slice(HEADS + k * EXPERTS, HEADS + (k + 1) * EXPERTS)
                s.did(dve.tensor_tensor(asum[:, :, e], node[:, :, H0 + k * EXPERTS:H0 + (k + 1) * EXPERTS],
                                        asum[:, :, k:k + 1].broadcast_to([P, B, EXPERTS]), ALU.mult))
            s.settle()
            s.step(dve.tensor_copy(ad, node[:, :, A_D:A_D + HEADS]))
            dve.nop().then_inc(s_m, 1)
            start = s.n
            with dve.Fori(0, T2 // GS) as i:
                l = Steps(dve, s_step, start + 6 * i)
                for h in range(2):
                    dve.wait_ge(s_mm, i * 2)
                    for j in range(h * G, (h + 1) * G):
                        dve.tensor_scalar(hot[:, j, :], lane[:], list2[:, bass.ds(i * GS + j, 1), 1], None,
                                          ALU.is_equal).then_inc(s_hot, 1)
                for h in range(2):
                    hs = slice(h * G, (h + 1) * G)
                    pe_ = p_e[h][:, 0:8 * G].rearrange("p (j w) -> p j w", w=8)
                    dve.wait_ge(s_e, i * 2 + h + 1)
                    l.step(dve.tensor_tensor(z[:, hs, :], gat[:, bass.ds(i * GS + h * G, G), 0:HEADS],
                                             pe_[:, :, 0:HEADS], ALU.add))
                    l.step(dve.scalar_tensor_tensor(out=z[:, hs, :], in0=z[:, hs, :], scalar=0.2, in1=z[:, hs, :],
                                                    op0=ALU.mult, op1=ALU.max))
                    l.step(dve.tensor_tensor(z[:, hs, :], z[:, hs, :], pe_[:, :, HEADS:2 * HEADS], ALU.subtract))
                    dve.tensor_scalar(z[:, hs, :], z[:, hs, :], 0.0, None, ALU.min).then_inc(s_zr, 1)
                for h in range(2):
                    dve.wait_ge(s_exp, i * 2 + h + 1)
                    hs = slice(h * G, (h + 1) * G)
                    for k in range(HEADS):
                        e = slice(HEADS + k * EXPERTS, HEADS + (k + 1) * EXPERTS)
                        mm = dve.tensor_tensor(val[:, hs, e], gat[:, bass.ds(i * GS + h * G, G), e],
                                               val[:, hs, k:k + 1].broadcast_to([P, G, EXPERTS]), ALU.mult)
                        mm.then_inc(s_v4, 1)
                    dve.wait_ge(s_v4, (i * 2 + h + 1) * HEADS)
                    dve.nop().then_inc(s_val, 1)
                for h in range(2):
                    for j in range(G):
                        t = i * GS + h * G + j
                        b = dve.value_load(blk2[0:1, bass.ds(t, 1)], min_val=0, max_val=B - 1)
                        a = asum[:, bass.ds(b, 1), :].rearrange("p o w -> p (o w)")
                        dve.wait_ge(s_mm, i * 2 + h + 1)
                        dve.wait_ge(s_sum, t)
                        dve.tensor_tensor(a, a, p_s[h][:, j * K:(j + 1) * K], ALU.add).then_inc(s_sum, 1)
            s.n = start + 6 * (T2 // GS)
            dve.wait_ge(s_sum, T2)
            s.step(dve.tensor_scalar(asum[:, :, 0:HEADS], asum[:, :, 0:HEADS], 1e-16, None, ALU.add))
            s.step(dve.reciprocal(asum[:, :, 0:HEADS], asum[:, :, 0:HEADS]))
            for k in range(HEADS):
                s.did(dve.tensor_tensor(agg[:, :, k * EXPERTS:(k + 1) * EXPERTS],
                                        asum[:, :, HEADS + k * EXPERTS:HEADS + (k + 1) * EXPERTS],
                                        asum[:, :, k:k + 1].broadcast_to([P, B, EXPERTS]), ALU.mult))
            dve.wait_ge(s_ld, 48)
            s.settle()

            def row(n):
                return rowc[:, n, :].unsqueeze(1).broadcast_to([P, B, HE])

            def wide(v):
                return v[:].unsqueeze(2).broadcast_to([P, B, HE])

            s.step(dve.tensor_tensor(agg, agg, row(0), ALU.add))
            s.step(dve.tensor_reduce(mu[:], agg, AX.X, ALU.add))
            s.step(dve.tensor_scalar(mu[:], mu[:], 1.0 / HE, None, ALU.mult))
            s.step(dve.tensor_tensor(agg, agg, wide(mu), ALU.subtract))
            s.step(dve.tensor_tensor(sq, agg, agg, ALU.mult))
            s.step(dve.tensor_reduce(var[:], sq, AX.X, ALU.add))
            s.step(dve.tensor_scalar(var[:], var[:], 1.0 / HE, None, ALU.mult))
            dve.nop().then_inc(s_a, 1)
            dve.wait_ge(s_b, 2)
            s.step(dve.reciprocal(var[:], var[:]))
            s.step(dve.tensor_tensor(agg, agg, wide(var), ALU.mult))
            s.step(dve.tensor_tensor(agg, agg, row(1), ALU.mult))
            s.step(dve.tensor_tensor(agg, agg, row(2), ALU.add))
            s.step(dve.tensor_reduce(sc[:], agg.rearrange("p b (h e) -> p b e h", h=HEADS), AX.X, ALU.add))
            s.step(dve.tensor_scalar(sc[:], sc[:], 1.0 / HEADS, None, ALU.mult))
            s.step(dve.memset(rank_[:], 0.0))
            for a in range(EXPERTS):
                for o in range(EXPERTS):
                    if o != a:
                        s.step(dve.tensor_tensor(less[:], sc[:, :, o], sc[:, :, a], ALU.is_ge if o < a else ALU.is_gt))
                        s.step(dve.tensor_tensor(rank_[:, :, a], rank_[:, :, a], less[:], ALU.add))
            s.step(dve.tensor_reduce(top[:], sc[:], AX.X, ALU.max))
            s.step(dve.tensor_tensor(sc[:], sc[:], top[:].unsqueeze(2).broadcast_to([P, B, EXPERTS]), ALU.subtract))
            dve.nop().then_inc(s_a, 1)
            s.step(dve.tensor_scalar(rank_[:], rank_[:], 2.0, None, ALU.is_lt))
            dve.wait_ge(s_b, 3)
            s.step(dve.tensor_tensor(gate[:], gate[:], rank_[:], ALU.mult))
            s.step(dve.tensor_reduce(top[:], gate[:], AX.X, ALU.add))
            s.step(dve.reciprocal(top[:], top[:]))
            s.step(dve.tensor_tensor(gate[:], gate[:], top[:].unsqueeze(2).broadcast_to([P, B, EXPERTS]), ALU.mult))

    if stop_after == 3:
        debug(nc, locals())
        ctx.close()
        return

    with ExitStack() as c6:
        def sem6(name):
            return c6.enter_context(nc.semaphore(name))

        def ps6(name):
            return c6.enter_context(nc.psum_tensor(name, [P, 512], F32))

        at = [0]

        def part(*shape):
            n = 1
            for v in shape:
                n *= v
            v = big[:, at[0]:at[0] + n]
            at[0] += n
            return v

        TG = 4
        W1 = part(EXPERTS * 2 * FH).rearrange("p (e c n) -> p e c n", e=EXPERTS, c=2)
        W2 = part(EXPERTS * FC * D).rearrange("p (e f n) -> p e f n", e=EXPERTS, f=FC)
        b1c = part(EXPERTS * FC)
        xn = part(TG * D).rearrange("p (t d) -> p t d", t=TG)
        xt = part(2 * TG * P).rearrange("p (c n) -> p c n", c=2)
        hT = part(2 * FC * TG * P).rearrange("p (w f n) -> p w f n", w=2, f=FC)
        b2r = part(EXPERTS * D)
        p_t = [ps6("f_t0"), ps6("f_t1")]
        p_h = [ps6("f_h0"), ps6("f_h1")]
        p_y = [ps6(f"f_y{j}") for j in range(TG)]
        f_ld, f_xn, f_tp, f_xt, f_h, f_g, f_y, f_add, f_out = (
            sem6(n) for n in ("f_ld", "f_xn", "f_tp", "f_xt", "f_h", "f_g", "f_y", "f_add", "f_out"))
        n_group = FULL // TG
        assert n_group * TG == FULL and LAST
        block = c6.enter_context(nc.Block())

        @block.sync
        def _(sp):
            for e in range(EXPERTS):
                sp.dma_start(W1[:, e], fW1[e].rearrange("(c p) n -> p c n", p=P)).then_inc(f_ld, 16)
                sp.dma_start(W2[:, e], fW2[e].rearrange("(f p) n -> p f n", p=P)).then_inc(f_ld, 16)
                for f in range(FC):
                    sp.dma_start(b1c[:, e * FC + f:e * FC + f + 1],
                                 fb1[e, f * P:(f + 1) * P].rearrange("(p o) -> p o", o=1)).then_inc(f_ld, 16)
            sp.dma_start(b2r[0:1, :], fb2.rearrange("e d -> (e d)").unsqueeze(0)).then_inc(f_ld, 16)
            with sp.Fori(0, n_group) as g:
                sp.wait_ge(f_add, g * (EXPERTS * TG) + EXPERTS * TG)
                sp.dma_start(out[bass.ds(g * (TG * P), TG * P), :].rearrange("(t p) d -> p t d", p=P),
                             res[:, bass.ds(g * TG, TG), :]).then_inc(f_out, 16)
            sp.wait_ge(f_add, n_group * EXPERTS * TG + EXPERTS)
            sp.dma_start(out[FULL * P:, :], res[0:LAST, FULL, :]).then_inc(f_out, 16)
            sp.wait_ge(f_out, 16 * (n_group + 1))

        N_LD = 16 * (EXPERTS * (2 + FC) + 1)

        def over_groups(eng, body):
            with eng.Fori(0, n_group) as g:
                body(g, TG)
            body(n_group, 1)

        @block.vector
        def _(dve):
            def body(g, nt):
                for t in range(nt):
                    dve.wait_ge(f_tp, g)
                    dve.tensor_scalar(xn[:, t, :], res[:, bass.ds(g * TG + t, 1), :].rearrange("p o d -> p (o d)"),
                                      mean[:, bass.ds(g * TG + t, 1), 0:1].rearrange("p o w -> p (o w)"),
                                      rstd[:, bass.ds(g * TG + t, 1)], ALU.subtract, ALU.mult).then_inc(f_xn, 1)
                for e in range(EXPERTS):
                    for t in range(nt):
                        b = g * TG + t
                        r = res[:, bass.ds(b, 1), :].rearrange("p o d -> p (o d)")
                        n = g * (EXPERTS * TG) + e * nt + t + 1
                        dve.wait_ge(f_y, n)
                        if e:
                            dve.wait_ge(f_add, n - nt)
                        else:
                            dve.wait_ge(f_xn, g * TG + nt)
                        dve.scalar_tensor_tensor(out=r, in0=p_y[t][:, 0:D],
                                                 scalar=gate[:, bass.ds(b, 1), e:e + 1].rearrange("p o w -> p (o w)"),
                                                 in1=r, op0=ALU.mult, op1=ALU.add).then_inc(f_add, 1)

            over_groups(dve, body)

        @block.scalar
        def _(act):
            act.wait_ge(f_ld, N_LD)

            def body(g, nt):
                act.wait_ge(f_tp, g + 1)
                for c in range(2):
                    nc.scalar.copy(xt[:, c, 0:nt * P], p_t[c][:, 0:nt * P]).then_inc(f_xt, 1)
                for e in range(EXPERTS):
                    for f in range(FC):
                        n = g * (EXPERTS * FC) + e * FC + f + 1
                        act.wait_ge(f_h, n)
                        if e >= 2:
                            act.wait_ge(f_y, g * (EXPERTS * TG) + (e - 1) * nt)
                        nc.scalar.activation(hT[:, e % 2, f, 0:nt * P], p_h[f % 2][:, 0:nt * P], ACT.Gelu,
                                             bias=b1c[:, e * FC + f:e * FC + f + 1]).then_inc(f_g, 1)

            over_groups(act, body)

        @block.tensor
        def _(pe):
            pe.wait_ge(f_ld, N_LD)

            def body(g, nt):
                pe.wait_ge(f_xn, g * TG + nt)
                pe.wait_ge(f_y, g * (EXPERTS * TG))
                for c in range(2):
                    for t in range(nt):
                        mm = nc.tensor.transpose(p_t[c][:, t * P:(t + 1) * P], xn[:, t, c * P:(c + 1) * P], ident[:])
                mm.then_inc(f_tp, 1)
                pe.wait_ge(f_xt, 2 * g + 2)

                def up(e):
                    for f in range(FC):
                        n = g * (EXPERTS * FC) + e * FC + f
                        if e or f >= 2:
                            pe.wait_ge(f_g, n - 1)
                        for c in range(2):
                            mm = nc.tensor.matmul(p_h[f % 2][:, 0:nt * P], W1[:, e, c, f * P:(f + 1) * P],
                                                  xt[:, c, 0:nt * P], start=(c == 0), stop=(c == 1))
                        mm.then_inc(f_h, 1)

                def down(e):
                    pe.wait_ge(f_g, g * (EXPERTS * FC) + (e + 1) * FC)
                    for t in range(nt):
                        if e:
                            pe.wait_ge(f_add, g * (EXPERTS * TG) + (e - 1) * nt + t + 1)
                        else:
                            pe.wait_ge(f_add, g * (EXPERTS * TG))
                        for f in range(FC):
                            nc.tensor.matmul(p_y[t][:, 0:D], hT[:, e % 2, f, t * P:(t + 1) * P], W2[:, e, f, :],
                                             start=(f == 0), stop=False)
                        nc.tensor.matmul(p_y[t][:, 0:D], ones[0:1, :], b2r[0:1, e * D:(e + 1) * D],
                                         start=False, stop=True).then_inc(f_y, 1)

                up(0)
                for e in range(1, EXPERTS):
                    up(e)
                    down(e - 1)
                down(EXPERTS - 1)

            over_groups(pe, body)

    ctx.close()


_INS = ['x', 'src', 'dst', 'L0_gnn_W1', 'L0_gnn_b1', 'L0_gnn_W2', 'L0_gnn_b2', 'L0_mix_wq', 'L0_mix_bq', 'L0_mix_wk',
        'L0_mix_bk', 'L0_mix_wv', 'L0_mix_bv', 'L0_mix_wo', 'L0_mix_bo', 'L0_ffn_W_gat', 'L0_ffn_att_src',
        'L0_ffn_att_dst', 'L0_ffn_b_gat', 'L0_ffn_ln_gamma', 'L0_ffn_ln_beta', 'L0_ffn_W1', 'L0_ffn_b1', 'L0_ffn_W2',
        'L0_ffn_b2', 'L0_ffn_edge_index']


def kernel(**inputs):
    import numpy as _np
    import concourse.bacc as _bacc
    from concourse import mybir as _mybir
    from concourse.bass_utils import run_bass_kernel_spmd as _run

    nc = _bacc.Bacc("TRN2", target_bir_lowering=False, num_devices=1)
    arrays, args = {}, []
    for name in _INS:
        a = _np.ascontiguousarray(inputs[name])
        arrays[f"in_{name}_dram"] = a
        args.append(nc.dram_tensor(f"in_{name}_dram", a.shape, _mybir.dt.from_np(a.dtype), kind="ExternalInput").ap())
    args.append(nc.dram_tensor("out_0_dram", inputs["x"].shape, F32, kind="ExternalOutput").ap())
    gps_kernel(nc, *args)
    r = _run(nc, [arrays], core_ids=[0])
    return r.results[0]["out_0_dram"]
```

```python
from contextlib import ExitStack

import concourse.bass as bass
from concourse import mybir

ALU = mybir.AluOpType
ACT = mybir.ActivationFunctionType
AX = mybir.AxisListType
F32 = mybir.dt.float32
I32 = mybir.dt.int32
BF16 = mybir.dt.bfloat16

P = 128
FARTHEST = 2.0 ** 110
LN_EPS = 1e-5
FAR = float(1 << 20)


class Steps:

    def __init__(self, eng, sem, base=0):
        self.eng, self.sem, self.n = eng, sem, base

    def did(self, ins):
        ins.then_inc(self.sem, 1)
        self.n = self.n + 1

    def settle(self):
        self.eng.wait_ge(self.sem, self.n)

    def step(self, ins):
        self.did(ins)
        self.settle()


def after(eng, sem, count):
    if not isinstance(count, int) or count > 0:
        eng.wait_ge(sem, count)


def rounds(eng, total, body):
    body(0)
    with eng.Fori(1, total) as i:
        body(i)


STEPS = 4


def pipeline(eng, total, drain, step):
    for i in range(2):
        for s in range(STEPS):
            step(i, s)
    with eng.Fori(2, total // STEPS) as i:
        for s in range(STEPS):
            step(i, s)
    for s in range(drain):
        step(total // STEPS, s)


def behind(i, s, lag, total):
    if s < lag:
        i, s = i - 1, s + STEPS
    s -= lag
    if isinstance(i, int) and not 0 <= STEPS * i + s < total:
        return None
    return i, s


def places(nc, eng, row, n, count, last):
    return nc.values_load_multi_w_load_instructions(
        row[0:1, bass.ds(n, count)], engines=[eng.engine], min_val=0, max_val=last,
        skip_runtime_bounds_check_because="the row is clamped to the last block where it is made")[1]


class EdgeList:

    def __init__(self, parts, cols, unroll, blocks, group):
        self.parts, self.cols, self.unroll = parts, cols, unroll
        tiles = (parts * cols + (P - 1) * blocks) // P
        self.tiles = -(-tiles // group) * group
        assert cols % (2 * unroll) == 0


def gps_kernel(nc, x, src, dst, gW1, gb1, gW2, gb2, wq, bq, wk, bk, wv, bv, wo, bo, W_gat, att_src, att_dst,
               b_gat, ln_gamma, ln_beta, fW1, fb1, fW2, fb2, edge_index, out):
    N, D = x.shape
    B = -(-N // P)
    FULL = N // P
    LAST = N - FULL * P
    NP = B * P
    HID = gW1.shape[1]
    YW = D + 1
    HEADS, EXPERTS = att_src.shape
    HE = HEADS * EXPERTS
    RW = 4 * HEADS + HE
    KW = HEADS + HE
    SW = 3 * HEADS + HE
    MH = 8
    MD = D // MH
    FH = fW1.shape[2]
    FC = FH // P
    Q = 4
    G = STEPS * Q
    E1 = EdgeList(125, src.shape[0] // 125, 5, B, G)
    E2 = EdgeList(P, edge_index.shape[1] // P, 16, B, G)
    assert 125 * E1.cols == src.shape[0] and P * E2.cols == edge_index.shape[1]
    T1, T2 = E1.tiles, E2.tiles

    ctx = ExitStack()

    def sb(name, shape, dt=F32):
        return ctx.enter_context(nc.sbuf_tensor(name, shape, dt))

    def ps(name, shape, dt=F32):
        return ctx.enter_context(nc.psum_tensor(name, shape, dt))

    def sem(name):
        return ctx.enter_context(nc.semaphore(name))

    def dram(name, shape, dt=F32):
        return nc.dram_tensor(name, shape, dt, kind="Internal").ap()

    list1_dram = dram("list1_dram", [P * T1, 2])
    list2_dram = dram("list2_dram", [P * T2, 2])
    y_dram = dram("y_dram", [NP, YW])
    node_dram = dram("node_dram", [NP, RW])
    rec2_dram = dram("rec2_dram", [P, E2.cols, 2])
    slot2_dram = dram("slot2_dram", [P, E2.cols], I32)

    res = sb("res", [P, B, D])
    big = sb("big", [P, 2 * B * P + B * YW])
    list1 = sb("list1", [P, T1, 2])
    list2 = sb("list2", [P, T2 + G, 2])
    blk1 = sb("blk1", [1, T1], I32)
    blk2 = sb("blk2", [1, T2], I32)
    ident = sb("ident", [P, P])
    ones = sb("ones", [P, P])
    before = sb("before", [P, P])
    lane = sb("lane", [P, P])
    valid = sb("valid", [P, B])
    epsc = sb("epsc", [P, 1])
    mean = sb("mean", [P, B, 2])
    rstd = sb("rstd", [P, B])
    bst = sb("bst", [P, B, 6])
    own_flat = sb("own", [P, B * SW])
    kv = own_flat[:, 0:2 * P].rearrange("p (c n) -> p c n", c=2)
    ks = own_flat[:, 2 * P:4 * P].rearrange("p (c n) -> p c n", c=2)
    recring = sb("recring", [P, 2, 16, 2])
    slotring = sb("slotring", [P, 2, 16], I32)
    ring_full = [sem("ring0_full"), sem("ring1_full")]
    half_out = [sem("half0_out"), sem("half1_out")]
    identb = sb("identb", [P, P], BF16)
    laneb = sb("laneb", [P, P], BF16)
    zero1, turn = sb("zero1", [1, 1]), sb("turn", [1, 1])
    turned, turns = sem("turned"), [0]
    y_stored, node_stored = sem("y_stored"), sem("node_stored")

    XNT = 2 * B * P
    xnT = big[:, 0:XNT].rearrange("p (c n) -> p c n", c=2)
    acc = big[:, XNT:].rearrange("p (b w) -> p b w", w=YW)
    gat = big[:, 0:T2 * KW].rearrange("p (t w) -> p t w", w=KW)

    def fill_rings(sp, g, records, slots):
        E = (E1, E2)[g]
        U, q = E.unroll, E.parts

        def body(i):
            for half in range(2):
                after(sp, half_out[half], i * (16 * U) + (0 if g == 0 else 8 * E1.cols))
                c0 = i * (2 * U) + half * U
                sp.dma_start(recring[0:q, half, 0:U, :], records[0:q, bass.ds(c0, U), :]).then_inc(ring_full[half], 16)
                sp.dma_start(slotring[0:q, half, 0:U], slots[0:q, bass.ds(c0, U)]).then_inc(ring_full[half], 16)

        rounds(sp, E.cols // (2 * U), body)

    def scatter(pool, g, target):
        E = (E1, E2)[g]
        U, n_loop, filled = E.unroll, E.cols // (2 * E.unroll), 0 if g == 0 else 32 * (E1.cols // (2 * E1.unroll))
        last_row = pool.to_reg(P * E.tiles - 1)

        def body(i):
            for half in range(2):
                pool.wait_ge(ring_full[half], filled + i * 32 + 32)
                after(pool, turned, turns[0] + 2 * i + half)
                pool.tensor_tensor(turn[:], zero1[:], zero1[:], ALU.add).then_inc(turned, 1)
                for u in range(U):
                    pool.indirect_dma_start(
                        target, bass.IndirectOffsetOnAxis(ap=slotring[0:E.parts, half, u:u + 1], axis=0),
                        recring[0:E.parts, half, u, :], None,
                        bounds_check=last_row, oob_is_err=False).then_inc(half_out[half], 16)

        rounds(pool, n_loop, body)
        turns[0] += 2 * n_loop

    with ExitStack() as c1:
        def sb1(name, shape, dt=F32):
            return c1.enter_context(nc.sbuf_tensor(name, shape, dt))

        def ps1(name, shape, dt=F32):
            return c1.enter_context(nc.psum_tensor(name, shape, dt))

        def sem1(name):
            return c1.enter_context(nc.semaphore(name))

        at = [XNT]

        def scratch(*shape):
            n = 1
            for s in shape:
                n *= s
            v = big[:, at[0]:at[0] + n]
            at[0] += n
            assert at[0] <= XNT + B * YW
            return v

        C = max(E1.cols, E2.cols)
        mask, scan = scratch(C), scratch(C)
        key, slot = [scratch(E1.cols), scratch(E2.cols)], [scratch(E1.cols), scratch(E2.cols)]
        rec = [scratch(E1.cols * 2).rearrange("p (c w) -> p c w", w=2),
               scratch(E2.cols * 2).rearrange("p (c w) -> p c w", w=2)]
        raw_i = scratch(C).bitcast(I32)
        raw_j = scratch(C).bitcast(I32)
        empty = list2
        zrow = sb1("zrow", [1, 2 * (P + 1)])
        counts = sb1("counts", [P, B])
        cnt_i = sb1("cnt_i", [P, B], I32)
        ntile = sb1("ntile", [P, B])
        tend = sb1("tend", [P, B])
        off = sb1("off", [P, B])
        bsum = sb1("bsum", [P, B])
        tend_c = sb1("tend_c", [P, 1])

        W1s = sb1("W1s", [P, 2, HID])
        W2s = sb1("W2s", [P, 1])
        b1s = sb1("b1s", [P, 1])
        b2s = sb1("b2s", [1, 1])
        wks = sb1("wks", [P, 2, D])
        wvs = sb1("wvs", [P, 2, D])
        rows = sb1("rows", [1, 2, D])
        xn = sb1("xn", [P, D])
        xt = sb1("xt", [P, 2, P])
        hT = sb1("hT", [P, P])
        kmin = sb1("kmin", [P, D])
        kexp = sb1("kexp", [P, D])
        kf = sb1("kf", [P, D])
        vt = sb1("vt", [P, 2, P + 1])
        wexp = sb1("wexp", [P, 2])
        scale = sb1("scale", [P, 1])
        yt = sb1("yt", [P, YW])

        p_tp = ps1("p_tp", [P, 512])
        p_h = ps1("p_h", [P, 512])
        p_k = ps1("p_k", [P, 512])
        p_v = ps1("p_v", [P, 512])
        p_z = ps1("p_z", [P, 512])
        p_kv = ps1("p_kv", [P, 512])
        p_cnt = ps1("p_cnt", [P, 512])
        p_blk = ps1("p_blk", [P, 512])
        kv_acc = p_kv[:, 0:2 * (P + 1)].rearrange("p (c w) -> p c w", c=2)

        loaded, made, x_in, res_zero = sem1("loaded"), sem1("made"), sem1("x_in"), sem1("res_zero")
        ids_in = [sem1("ids1_in"), sem1("ids2_in")]
        dve_done = sem1("dve_done")
        ids_free = sem1("ids_free")
        iota_made = sem1("iota_made")
        counts_ready, sums_ready = sem1("counts_ready"), sem1("sums_ready")
        ge_ready, blk_ready, blk_taken = sem1("ge_ready"), sem1("blk_ready"), sem1("blk_taken")
        slots_ready, empty_made, empty_in = sem1("slots_ready"), sem1("empty_made"), sem1("empty_in")
        a_xn, a_tp, a_xt, a_mm, a_h, a_z = (sem1(n) for n in ("a_xn", "a_tp", "a_xt", "a_mm", "a_h", "a_z"))
        a_min, a_exp, a_kv, a_wexp, a_y, a_kvdone = (sem1(n) for n in ("a_min", "a_exp", "a_kv", "a_wexp", "a_y", "a_kvdone"))
        y_out, kv_zero, kv_all = sem1("y_out"), sem1("kv_zero"), sem1("kv_all")
        var_ready, sd_ready = sem1("var_ready"), sem1("sd_ready")
        a_scale = sem1("a_scale")
        list1_in, rec2_out = sem1("list1_in"), sem1("rec2_out")

        N_LD = 16 * 8
        block = c1.enter_context(nc.Block())
        EDGES = ((E1, src.rearrange("(p c) -> p c", p=E1.parts), dst.rearrange("(p c) -> p c", p=E1.parts), True),
                 (E2, edge_index[0].rearrange("(p c) -> p c", p=P), edge_index[1].rearrange("(p c) -> p c", p=P), False))

        @block.sync
        def _(sp):
            sp.dma_start(raw_i[0:E1.parts, 0:E1.cols], EDGES[0][1]).then_inc(ids_in[0], 16)
            sp.dma_start(raw_j[0:E1.parts, 0:E1.cols], EDGES[0][2]).then_inc(ids_in[0], 16)
            sp.dma_start(res[:, 0:FULL, :], x[0:FULL * P].rearrange("(b p) d -> p b d", p=P)).then_inc(x_in, 16)
            sp.wait_ge(res_zero, 1)
            sp.dma_start(res[0:LAST, FULL, :], x[FULL * P:]).then_inc(x_in, 16)
            for w, a in ((W1s, gW1), (wks, wk), (wvs, wv)):
                sp.dma_start(w[:], a.rearrange("(c p) n -> p c n", p=P)).then_inc(loaded, 16)
            sp.dma_start(W2s[:], gW2).then_inc(loaded, 16)
            sp.dma_start(b1s[:], gb1.rearrange("(p o) -> p o", o=1)).then_inc(loaded, 16)
            sp.dma_start(b2s[:], gb2.rearrange("(p o) -> p o", o=1)).then_inc(loaded, 16)
            for n, a in enumerate((bk, bv)):
                sp.dma_start(rows[:, n, :], a.rearrange("(o d) -> o d", o=1)).then_inc(loaded, 16)
            sp.wait_ge(empty_made, 2)
            sp.dma_start(list1_dram.rearrange("(p t) w -> p t w", p=P), empty[:, 0:T1, :]).then_inc(empty_in, 16)
            sp.dma_start(list2_dram.rearrange("(p t) w -> p t w", p=P), empty[:, 0:T2, :]).then_inc(empty_in, 16)
            sp.wait_ge(ids_free, 1)
            sp.dma_start(raw_i[:, 0:E2.cols], EDGES[1][1]).then_inc(ids_in[1], 16)
            sp.dma_start(raw_j[:, 0:E2.cols], EDGES[1][2]).then_inc(ids_in[1], 16)
            sp.wait_ge(slots_ready, 1)
            fill_rings(sp, 0, rec[0], key[0].bitcast(I32))
            sp.wait_ge(slots_ready, 2)
            sp.dma_start(rec2_dram, rec[1]).then_inc(rec2_out, 16)
            sp.dma_start(slot2_dram, key[1].bitcast(I32)).then_inc(rec2_out, 16)
            for half in range(2):
                sp.wait_ge(half_out[half], 8 * E1.cols)
            sp.dma_start(list1[:], list1_dram.rearrange("(p t) w -> p t w", p=P)).then_inc(list1_in, 16)
            sp.wait_ge(list1_in, 16)
            sp.wait_ge(rec2_out, 32)

        @block.gpsimd
        def _(pool):
            pool.memset(zero1[:], 0.0).then_inc(made, 1)
            pool.memset(res[:, FULL, :], 0.0).then_inc(res_zero, 1)
            pool.iota(lane[:], [[1, P]], base=0, channel_multiplier=0,
                      allow_small_or_imprecise_dtypes=True).then_inc(iota_made, 1)
            pool.memset(empty[:, :, 0], 0.0).then_inc(empty_made, 1)
            pool.memset(empty[:, :, 1], -1.0).then_inc(empty_made, 1)
            pool.memset(ones[:], 1.0).then_inc(made, 1)
            pool.memset(ident[:], 0.0).then_inc(made, 1)
            pool.memset(valid[:], 1.0).then_inc(made, 1)
            pool.memset(zrow[:], 0.0).then_inc(made, 1)
            pool.wait_ge(made, 5)
            pool.affine_select(out=ident[:], in_=ident[:], compare_op=ALU.not_equal, fill=1.0, base=0,
                               pattern=[[-1, P]], channel_multiplier=1).then_inc(made, 1)
            pool.affine_select(out=before[:], in_=ones[:], compare_op=ALU.is_gt, fill=0.0, base=0,
                               pattern=[[1, P]], channel_multiplier=-1).then_inc(made, 1)
            pool.affine_select(out=valid[:], in_=valid[:], compare_op=ALU.is_ge, fill=0.0, base=N - 1,
                               pattern=[[-P, B]], channel_multiplier=-1).then_inc(made, 1)
            pool.wait_ge(empty_in, 32)
            scatter(pool, 0, list1_dram)

        @block.vector
        def _(dve):
            s = Steps(dve, dve_done)

            def rank(g):
                E, _, _, swapped = EDGES[g]
                q, Cn, T = E.parts, E.cols, E.tiles
                k, r, e = key[g][0:q], slot[g][0:q], rec[g]
                m, sc = mask[0:q, 0:Cn], scan[0:q, 0:Cn]
                source, target = (raw_j, raw_i) if swapped else (raw_i, raw_j)
                source, target = source[0:q, 0:Cn], target[0:q, 0:Cn]
                dve.wait_ge(ids_in[g], 32)
                s.step(dve.memset(counts[:], 0.0))
                s.did(dve.tensor_scalar(sc.bitcast(I32), target, 7, None, ALU.logical_shift_right))
                s.did(dve.tensor_scalar(m.bitcast(I32), target, P - 1, None, ALU.bitwise_and))
                s.did(dve.tensor_scalar(e[0:q, :, 0], source, float(N - 1), None, ALU.min))
                s.settle()
                s.did(dve.tensor_copy(k, sc.bitcast(I32)))
                s.step(dve.tensor_copy(e[0:q, :, 1], m.bitcast(I32)))
                s.did(dve.tensor_scalar(r, k, float(B), FAR, ALU.is_ge, ALU.mult))
                if g == 0:
                    dve.nop().then_inc(ids_free, 1)
                s.settle()
                start = s.n
                with dve.Fori(0, B) as b:
                    l = Steps(dve, dve_done, start + b * 5)
                    l.step(dve.tensor_scalar(m, k, lane[0:q, bass.ds(b, 1)], None, ALU.is_equal))
                    l.step(dve.tensor_tensor_scan(sc, m, m, 0.0, ALU.add, ALU.max))
                    l.step(dve.tensor_copy(counts[0:q, bass.ds(b, 1)], sc[:, Cn - 1:Cn]))
                    l.step(dve.tensor_tensor(sc, sc, m, ALU.mult))
                    l.step(dve.tensor_tensor(r, r, sc, ALU.add))
                s.n = start + B * 5
                dve.nop().then_inc(counts_ready, 1)
                dve.wait_ge(sums_ready, g + 1)
                s.step(dve.tensor_copy(cnt_i[:], p_cnt[:, B:2 * B]))
                s.step(dve.tensor_scalar(cnt_i[:], cnt_i[:], float(P - 1), None, ALU.add))
                s.step(dve.tensor_scalar(cnt_i[:], cnt_i[:], 7, None, ALU.logical_shift_right))
                s.step(dve.tensor_copy(ntile[:], cnt_i[:]))
                s.step(dve.tensor_tensor_scan(tend[:], ntile[:], ntile[:], 0.0, ALU.add, ALU.max))
                s.step(dve.tensor_tensor(off[:], tend[:], ntile[:], ALU.subtract))
                s.step(dve.tensor_scalar(off[:], off[:], float(P), -1.0, ALU.mult, ALU.add))
                s.step(dve.tensor_tensor(off[:], off[:], p_cnt[:, 0:B], ALU.add))
                s.step(dve.tensor_tensor(bsum[0:B, :], tend[0:B, :], ident[0:B, 0:B], ALU.mult))
                s.step(dve.tensor_reduce(tend_c[0:B, :], bsum[0:B, :], AX.X, ALU.add))
                n_part = -(-T // 512)
                for part in range(n_part):
                    w = min(512, T - 512 * part)
                    for a in range(0, w, P):
                        z = min(P, w - a)
                        s.did(dve.tensor_scalar(mask[0:B, a:a + z], lane[0:B, 0:z], float(512 * part + a),
                                                tend_c[0:B, 0:1], ALU.add, ALU.is_ge))
                    s.settle()
                    dve.nop().then_inc(ge_ready, 1)
                    dve.wait_ge(blk_ready, blk_done[0] + 1)
                    blk_done[0] += 1
                    s.step(dve.tensor_scalar((blk1, blk2)[g][0:1, 512 * part:512 * part + w], p_blk[0:1, 0:w],
                                             float(B - 1), float((YW, SW)[g]), ALU.min, ALU.mult))
                start = s.n
                with dve.Fori(0, B) as b:
                    l = Steps(dve, dve_done, start + b * 2)
                    l.step(dve.tensor_scalar(m, k, lane[0:q, bass.ds(b, 1)], None, ALU.is_equal))
                    l.step(dve.scalar_tensor_tensor(out=r, in0=m, scalar=off[0:q, bass.ds(b, 1)], in1=r,
                                                    op0=ALU.mult, op1=ALU.add))
                s.n = start + B * 2
                s.step(dve.tensor_copy(sc.bitcast(I32), r))
                s.did(dve.tensor_scalar(m.bitcast(I32), sc.bitcast(I32), P - 1, None, ALU.bitwise_and))
                s.step(dve.tensor_scalar(k.bitcast(I32), sc.bitcast(I32), 7, None, ALU.logical_shift_right))
                s.did(dve.tensor_copy(r, m.bitcast(I32)))
                s.step(dve.tensor_copy(sc, k.bitcast(I32)))
                s.step(dve.scalar_tensor_tensor(out=r, in0=r, scalar=float(T), in1=sc, op0=ALU.mult, op1=ALU.add))
                s.step(dve.tensor_scalar(m, sc, float(T), FAR, ALU.is_ge, ALU.mult))
                s.step(dve.tensor_tensor(r, r, m, ALU.add))
                s.step(dve.tensor_copy(k.bitcast(I32), r))
                dve.nop().then_inc(slots_ready, 1)

            blk_done = [0]
            dve.wait_ge(iota_made, 1)
            dve.wait_ge(made, 8)
            rank(0)
            rank(1)

            s.step(dve.memset(epsc[:], LN_EPS))
            dve.wait_ge(x_in, 32)
            start = s.n
            with dve.Fori(0, B) as b:
                dve.bn_stats(bst[:, bass.ds(b, 1), :].rearrange("p o w -> p (o w)"),
                             res[:, bass.ds(b, 1), :].rearrange("p o d -> p (o d)")).then_inc(dve_done, 1)
            s.n = start + B
            s.settle()
            for b in range(B):
                s.did(dve.bn_aggr(mean[:, b, :], bst[:, b, :]))
            s.settle()
            dve.nop().then_inc(var_ready, 1)
            dve.wait_ge(sd_ready, 1)
            s.step(dve.reciprocal(rstd[:], rstd[:]))

            start = s.n

            def normalize(b):
                dve.tensor_scalar(xn[:], res[:, bass.ds(b, 1), :].rearrange("p o d -> p (o d)"),
                                  mean[:, bass.ds(b, 1), 0:1].rearrange("p o w -> p (o w)"),
                                  rstd[:, bass.ds(b, 1)], ALU.subtract, ALU.mult).then_inc(a_xn, 1)

            def attend(b, more=True):
                l = Steps(dve, dve_done, start + 5 * b)
                if more:
                    dve.wait_ge(a_tp, b + 1)
                    normalize(b + 1)
                dve.wait_ge(a_mm, b + 1)
                dve.tensor_scalar(kmin[:], p_k[:, 0:D], 0.0, None, ALU.min).then_inc(a_min, 1)
                after(dve, a_kvdone, b)
                for c in range(2):
                    l.did(dve.tensor_scalar(vt[:, c, 0:P], p_v[:, c * P:(c + 1) * P], valid[:, bass.ds(b, 1)],
                                            None, ALU.mult))
                    dve.tensor_copy(vt[:, c, P:P + 1], valid[:, bass.ds(b, 1)]).then_inc(kv_zero, 1)
                dve.wait_ge(a_exp, b + 1)
                l.did(dve.scalar_tensor_tensor(out=kf[:], in0=p_k[:, 0:D], scalar=0.0, in1=kexp[:],
                                               op0=ALU.max, op1=ALU.add))
                l.settle()
                dve.nop().then_inc(a_kv, 1)
                after(dve, y_out, 16 * b)
                dve.wait_ge(a_wexp, b + 1)
                l.step(dve.tensor_scalar(wexp[:, 1:2], wexp[:, 0:1], 1.0, None, ALU.add))
                l.step(dve.reciprocal(yt[:, D:YW], wexp[:, 1:2]))
                dve.tensor_tensor(scale[:], yt[:, D:YW], rstd[:, bass.ds(b, 1)], ALU.mult).then_inc(a_scale, 1)
                dve.wait_ge(a_scale, b + 1)
                dve.tensor_scalar(yt[:, 0:D], res[:, bass.ds(b, 1), :].rearrange("p o d -> p (o d)"),
                                  mean[:, bass.ds(b, 1), 0:1].rearrange("p o w -> p (o w)"),
                                  scale[:], ALU.subtract, ALU.mult).then_inc(a_y, 1)

            normalize(0)
            rounds(dve, B - 1, attend)
            attend(B - 1, more=False)
            s.n = start + 5 * B

            dve.wait_ge(kv_all, 1)
            s.did(dve.memset(kv, 0.0))
            s.step(dve.memset(ks, 0.0))
            for c in range(2):
                for h in range(P // MD):
                    d = slice(h * MD, (h + 1) * MD)
                    s.did(dve.tensor_copy(kv[d, c, d], kv_acc[d, c, d]))
                    s.did(dve.tensor_scalar(ks[d, c, d], ones[d, d], kv_acc[d, c, P:P + 1], None, ALU.mult))
            s.settle()

        @block.scalar
        def _(act):
            act.wait_ge(var_ready, 1)
            nc.scalar.activation(rstd[:], mean[:, :, 1], ACT.Sqrt, bias=epsc[:, 0:1]).then_inc(sd_ready, 1)
            act.wait_ge(loaded, N_LD)

            def keep(b):
                act.wait_ge(a_tp, b + 1)
                t = p_tp[:, 0:D].rearrange("p (c n) -> p c n", c=2)
                nc.scalar.copy(xt[:], t).then_inc(a_xt, 1)
                nc.scalar.copy(xnT[:, :, bass.ds(b * P, P)], t).then_inc(a_xt, 1)

            def attend(b, more=True):
                act.wait_ge(a_mm, b + 1)
                nc.scalar.activation(hT[:], p_h[:, 0:P], ACT.Relu, bias=b1s[:, 0:1]).then_inc(a_h, 1)
                act.wait_ge(a_min, b + 1)
                nc.scalar.activation(kexp[:], kmin[:], ACT.Exp).then_inc(a_exp, 1)
                if more:
                    keep(b + 1)
                act.wait_ge(a_z, b + 1)
                nc.scalar.activation(wexp[:, 0:1], p_z[:, 0:1], ACT.Exp, scale=-1.0).then_inc(a_wexp, 1)
                act.wait_ge(a_y, b + 1)
                act.dma_start(y_dram[bass.ds(b * P, P), :], yt[:]).then_inc(y_out, 16)

            keep(0)
            rounds(act, B - 1, attend)
            attend(B - 1, more=False)
            act.wait_ge(y_out, 16 * B)
            act.nop().then_inc(y_stored, 1)
        @block.tensor
        def _(pe):
            blk_n = [0]

            def sums(g):
                T = EDGES[g][0].tiles
                pe.wait_ge(counts_ready, g + 1)
                nc.tensor.matmul(p_cnt[:, 0:B], before[:], counts[:], start=True, stop=True)
                nc.tensor.matmul(p_cnt[:, B:2 * B], ones[:], counts[:], start=True, stop=True).then_inc(sums_ready, 1)
                for part in range(-(-T // 512)):
                    w = min(512, T - 512 * part)
                    blk_n[0] += 1
                    pe.wait_ge(ge_ready, blk_n[0])
                    nc.tensor.matmul(p_blk[0:1, 0:w], ones[0:B, 0:1], mask[0:B, 0:w], start=True,
                                     stop=True).then_inc(blk_ready, 1)

            sums(0)
            sums(1)
            pe.wait_ge(loaded, N_LD)
            nc.tensor.matmul(kv_acc, zrow[:, 0:P], zrow[:], start=True, stop=False,
                             skip_group_check=True)

            def turn_over(b):
                pe.wait_ge(a_xn, b + 1)
                after(pe, a_xt, 2 * b)
                nc.tensor.transpose(p_tp[:, 0:P], xn[:, 0:P], ident[:])
                nc.tensor.transpose(p_tp[:, P:D], xn[:, P:D], ident[:]).then_inc(a_tp, 1)

            def attend(b, more=True):
                pe.wait_ge(a_xt, 2 * b + 1)
                for c in range(2):
                    nc.tensor.matmul(p_h[:, 0:P], W1s[:, c, :], xt[:, c, :], start=(c == 0), stop=(c == 1))
                for w, o, r in ((wks, p_k, 0), (wvs, p_v, 1)):
                    for c in range(2):
                        nc.tensor.matmul(o[:, 0:D], xt[:, c, :], w[:, c, :], start=(c == 0), stop=False)
                    last = nc.tensor.matmul(o[:, 0:D], ones[0:1, :], rows[0:1, r, :], start=False, stop=True)
                last.then_inc(a_mm, 1)
                if more:
                    turn_over(b + 1)
                pe.wait_ge(a_h, b + 1)
                after(pe, a_wexp, b)
                nc.tensor.matmul(p_z[:, 0:1], hT[:], W2s[:], start=True, stop=False)
                nc.tensor.matmul(p_z[:, 0:1], ones[0:1, :], b2s[:], start=False, stop=True).then_inc(a_z, 1)
                pe.wait_ge(a_kv, b + 1)
                pe.wait_ge(kv_zero, 2 * b + 2)
                for c in range(2):
                    last = nc.tensor.matmul(kv_acc[:, c, :], kf[:, c * P:(c + 1) * P], vt[:, c, :],
                                            start=False, stop=False, skip_group_check=True)
                last.then_inc(a_kvdone, 1)

            turn_over(0)
            rounds(pe, B - 1, attend)
            attend(B - 1, more=False)
            nc.tensor.matmul(kv_acc, zrow[:, 0:P], zrow[:], start=False, stop=True,
                             skip_group_check=True).then_inc(kv_all, 1)

    with ExitStack() as c2:
        def sb2(name, shape, dt=F32):
            return c2.enter_context(nc.sbuf_tensor(name, shape, dt))

        def sem2(name):
            return c2.enter_context(nc.semaphore(name))

        NQ = T1 // Q
        idx = sb2("g_idx", [P, G], I32)
        rowsg = sb2("g_rows", [P, G, YW])
        hot = sb2("g_hot", [P, G, P])
        p_sum = [c2.enter_context(nc.psum_tensor(f"g_sum{j}", [P, 512], F32)) for j in range(2 * Q)]
        g_zero, g_idx, g_hot, g_mm, g_sum = (sem2(n) for n in ("g_zero", "g_idx_ready", "g_hot_ready", "g_mm", "g_sum"))
        gath = [sem2(f"g_gath{s}") for s in range(STEPS)]
        block = c2.enter_context(nc.Block())

        @block.scalar
        def _(act):
            def step(i, s):
                after(act, gath[s], i * (16 * Q))
                nc.scalar.copy(idx[:, s * Q:(s + 1) * Q],
                               list1[:, bass.ds((i * STEPS + s) * Q, Q), 0]).then_inc(g_idx, 1)

            pipeline(act, NQ, 0, step)

        @block.gpsimd
        def _(pool):
            pool.wait_ge(y_stored, 1)

            def step(i, s):
                n = i * STEPS + s
                pool.wait_ge(g_idx, n + 1)
                after(pool, g_mm, (i - 1) * G + (s + 1) * Q)
                after(pool, turned, turns[0] + n)
                pool.tensor_tensor(turn[:], zero1[:], zero1[:], ALU.add).then_inc(turned, 1)
                for j in range(s * Q, (s + 1) * Q):
                    pool.indirect_dma_start(rowsg[:, j, :], None, y_dram,
                                            bass.IndirectOffsetOnAxis(ap=idx[:, j:j + 1], axis=0)
                                            ).then_inc(gath[s], 16)

            pipeline(pool, NQ, 0, step)
            turns[0] += NQ

        @block.tensor
        def _(pe):
            def step(i, s):
                pe.wait_ge(gath[s], i * (16 * Q) + 16 * Q)
                pe.wait_ge(g_hot, i * G + (s + 1) * Q)
                for j in range(s * Q, (s + 1) * Q):
                    after(pe, g_sum, i * G + j - 2 * Q + 1)
                    nc.tensor.matmul(p_sum[j % (2 * Q)][:, 0:YW], hot[:, j, :], rowsg[:, j, :],
                                     start=True, stop=True).then_inc(g_mm, 1)

            pipeline(pe, NQ, 0, step)

        @block.vector
        def _(dve):
            dve.memset(acc, 0.0).then_inc(g_zero, 1)
            dve.wait_ge(g_zero, 1)

            def step(i, s):
                if behind(i, s, 0, NQ):
                    after(dve, g_mm, (i - 1) * G + (s + 1) * Q)
                    for j in range(s * Q, (s + 1) * Q):
                        dve.tensor_scalar(hot[:, j, :], lane[:], list1[:, bass.ds(i * G + j, 1), 1], None,
                                          ALU.is_equal).then_inc(g_hot, 1)
                if last := behind(i, s, 1, NQ):
                    i, s = last
                    at = places(nc, dve, blk1, (i * STEPS + s) * Q, Q, (B - 1) * YW)
                    for j in range(s * Q, (s + 1) * Q):
                        t = i * G + j
                        a = big[:, XNT:][:, bass.ds(at[j % Q], YW)]
                        dve.wait_ge(g_mm, t + 1)
                        after(dve, g_sum, t)
                        dve.tensor_tensor(a, a, p_sum[j % (2 * Q)][:, 0:YW], ALU.add).then_inc(g_sum, 1)

            pipeline(dve, NQ, 1, step)

    node = sb("node", [P, B, RW + HEADS])
    own = own_flat[:].rearrange("p (b w) -> p b w", w=SW)
    vmax = own[:, :, HEADS:2 * HEADS]
    asum = own[:, :, 2 * HEADS:SW]
    gate = sb("gate", [P, B, EXPERTS])
    A_S, H0, A_D = 3 * HEADS, 4 * HEADS, 4 * HEADS + HE
    with ExitStack() as c3:
        def sb3(name, shape, dt=F32):
            return c3.enter_context(nc.sbuf_tensor(name, shape, dt))

        def sem3(name):
            return c3.enter_context(nc.semaphore(name))

        wqs = sb3("wqs", [P, 2, D])
        wos = sb3("wos", [P, 2, D])
        bqs = sb3("bqs", [P, 2])
        bos = sb3("bos", [1, D])
        qmin = sb3("qmin", [P, 2, P])
        qexp = sb3("qexp", [P, 2, P])
        qf = sb3("qf", [P, 2, P])
        oT = sb3("oT", [P, 2, P])
        p_q, p_o, p_l2, p_l3 = (c3.enter_context(nc.psum_tensor(n, [P, 512], F32)) for n in ("p_q", "p_o", "p_l2", "p_l3"))
        q_load, q_mm, q_min, q_exp, q_feat, q_att, q_o, q_mix, q_done, list2_in = (
            sem3(n) for n in ("q_load", "q_mm", "q_min", "q_exp", "q_feat", "q_att", "q_o", "q_mix", "q_done", "list2_in"))
        Wg = sb3("Wg", [P, 2, HE])
        att = sb3("att", [P, 2, HE])
        den = sb3("den", [P, B])
        xn = sb3("x_xn", [P, D])
        xt = sb3("x_xt", [P, 2, P])
        prod = sb3("x_prod", [P, 2, HE])
        left = sb3("left", [P, B, HEADS])
        rounded = sb3("rounded", [P, B, HEADS], BF16)
        p_t = c3.enter_context(nc.psum_tensor("x_pt", [P, 512], F32))
        p_g = c3.enter_context(nc.psum_tensor("x_pg", [P, 512], F32))
        x_load, x_done, x_var, x_sd = sem3("x_load"), sem3("x_done"), sem3("x_var"), sem3("x_sd")
        x_xn, x_tp, x_xt, x_h = sem3("x_xn_ready"), sem3("x_tp"), sem3("x_xt_ready"), sem3("x_h")
        x_node, x_out = sem3("x_node"), sem3("x_out")
        block = c3.enter_context(nc.Block())

        @block.sync
        def _(sp):
            for w, a in ((wqs, wq), (wos, wo)):
                sp.dma_start(w[:], a.rearrange("(c p) n -> p c n", p=P)).then_inc(q_load, 16)
            for c in range(2):
                sp.dma_start(bqs[:, c:c + 1], bq[c * P:(c + 1) * P].rearrange("(p o) -> p o", o=1)).then_inc(q_load, 16)
            sp.dma_start(bos[:], bo.rearrange("(o d) -> o d", o=1)).then_inc(q_load, 16)
            sp.dma_start(Wg[:], W_gat.rearrange("(c p) n -> p c n", p=P)).then_inc(x_load, 16)
            for n, a in enumerate((att_src, att_dst)):
                sp.dma_start(att[:, n, :], a.rearrange("h e -> (h e)").partition_broadcast(P)).then_inc(x_load, 16)
            fill_rings(sp, 1, rec2_dram, slot2_dram)
            sp.wait_ge(x_node, 1)
            sp.dma_start(node_dram.rearrange("(b p) w -> p b w", p=P), node[:, :, 0:RW]).then_inc(x_out, 16)
            sp.wait_ge(x_out, 16)
            sp.nop().then_inc(node_stored, 1)
            for half in range(2):
                sp.wait_ge(half_out[half], 8 * (E1.cols + E2.cols))
            sp.dma_start(list2[:, 0:T2, :], list2_dram.rearrange("(p t) w -> p t w", p=P)).then_inc(list2_in, 16)
            sp.wait_ge(list2_in, 16)

        @block.gpsimd
        def _(pool):
            scatter(pool, 1, list2_dram)

        @block.vector
        def _(dve):
            s = Steps(dve, x_done)
            dve.wait_ge(q_load, 16 * 5)
            start = s.n
            with dve.Fori(0, B) as b:
                l = Steps(dve, x_done, start + 5 * b)
                dve.wait_ge(q_mm, b + 1)
                for c in range(2):
                    l.did(dve.tensor_scalar(qmin[:, c, :], p_q[:, c * P:(c + 1) * P], bqs[:, c:c + 1], 0.0,
                                            ALU.add, ALU.min))
                l.settle()
                dve.nop().then_inc(q_min, 1)
                for c in range(2):
                    l.did(dve.tensor_scalar(qf[:, c, :], p_q[:, c * P:(c + 1) * P], bqs[:, c:c + 1], 0.0,
                                            ALU.add, ALU.max))
                l.settle()
                dve.wait_ge(q_exp, b + 1)
                dve.tensor_tensor(qf[:], qf[:], qexp[:], ALU.add).then_inc(q_feat, 1)
                dve.wait_ge(q_att, b + 1)
                l2 = p_l2[:, 0:2 * P].rearrange("p (c n) -> p c n", c=2)
                l3 = p_l3[:, 0:2 * P].rearrange("p (c n) -> p c n", c=2)
                l.step(dve.tensor_scalar(oT[:], l3, 1e-6, None, ALU.add))
                dve.reciprocal(oT[:], oT[:]).then_inc(q_o, 1)
                dve.wait_ge(q_o, 2 * b + 1)
                dve.tensor_tensor(oT[:], oT[:], l2, ALU.mult).then_inc(q_o, 1)
                dve.wait_ge(q_mix, b + 1)
                r = res[:, bass.ds(b, 1), :].rearrange("p o d -> p (o d)")
                dve.tensor_tensor(r, r, p_o[:, 0:D], ALU.add).then_inc(q_done, 1)
            s.n = start + 5 * B
            dve.wait_ge(q_done, B)
            s.step(dve.tensor_scalar(den[:], acc[:, :, D], 1e-12, None, ALU.max))
            s.step(dve.reciprocal(den[:], den[:]))
            start = s.n
            with dve.Fori(0, B) as b:
                r = res[:, bass.ds(b, 1), :].rearrange("p o d -> p (o d)")
                a = acc[:, bass.ds(b, 1), 0:D].rearrange("p o d -> p (o d)")
                dve.scalar_tensor_tensor(out=r, in0=a, scalar=den[:, bass.ds(b, 1)], in1=r,
                                         op0=ALU.mult, op1=ALU.add).then_inc(x_done, 1)
            s.n = start + B
            s.settle()
            with dve.Fori(0, B) as b:
                dve.bn_stats(bst[:, bass.ds(b, 1), :].rearrange("p o w -> p (o w)"),
                             res[:, bass.ds(b, 1), :].rearrange("p o d -> p (o d)")).then_inc(x_done, 1)
            s.n = start + 2 * B
            s.settle()
            for b in range(B):
                s.did(dve.bn_aggr(mean[:, b, :], bst[:, b, :]))
            s.settle()
            dve.nop().then_inc(x_var, 1)
            dve.wait_ge(x_sd, 1)
            s.step(dve.reciprocal(rstd[:], rstd[:]))
            dve.wait_ge(x_load, 48)
            start = s.n
            with dve.Fori(0, B) as b:
                l = Steps(dve, x_done, start + 4 * b)
                dve.tensor_scalar(xn[:], res[:, bass.ds(b, 1), :].rearrange("p o d -> p (o d)"),
                                  mean[:, bass.ds(b, 1), 0:1].rearrange("p o w -> p (o w)"),
                                  rstd[:, bass.ds(b, 1)], ALU.subtract, ALU.mult).then_inc(x_xn, 1)
                dve.wait_ge(x_h, b + 1)
                hb = p_g[:, 0:HE]
                nb = node[:, bass.ds(b, 1), :].rearrange("p o w -> p (o w)")
                l.did(dve.tensor_copy(nb[:, H0:H0 + HE], hb))
                l.step(dve.tensor_tensor(prod[:], att[:], hb.unsqueeze(1).broadcast_to([P, 2, HE]), ALU.mult))
                for n, o in enumerate((A_S, A_D)):
                    l.did(dve.tensor_reduce(nb[:, o:o + HEADS], prod[:, n, :].rearrange("p (h e) -> p h e", h=HEADS),
                                            AX.X, ALU.add))
                l.settle()
            s.n = start + 4 * B
            rest = node[:, :, A_S:A_S + HEADS]
            for c in range(3):
                part = node[:, :, c * HEADS:(c + 1) * HEADS]
                s.step(dve.tensor_copy(rounded[:], rest))
                s.step(dve.tensor_copy(part, rounded[:]))
                if c < 2:
                    s.step(dve.tensor_tensor(left[:], rest, part, ALU.subtract))
                    rest = left[:]
            dve.nop().then_inc(x_node, 1)
            s.did(dve.tensor_copy(identb[:], ident[:]))
            s.did(dve.tensor_copy(laneb[:], lane[:]))
            s.step(dve.tensor_copy(vmax, node[:, :, A_S:A_S + HEADS]))

        @block.scalar
        def _(act):
            with act.Fori(0, B) as b:
                act.wait_ge(q_min, b + 1)
                nc.scalar.activation(qexp[:], qmin[:], ACT.Exp).then_inc(q_exp, 1)
            act.wait_ge(x_var, 1)
            nc.scalar.activation(rstd[:], mean[:, :, 1], ACT.Sqrt, bias=epsc[:, 0:1]).then_inc(x_sd, 1)
            with act.Fori(0, B) as b:
                act.wait_ge(x_tp, b + 1)
                nc.scalar.copy(xt[:], p_t[:, 0:D].rearrange("p (c n) -> p c n", c=2)).then_inc(x_xt, 1)

        @block.tensor
        def _(pe):
            pe.wait_ge(q_load, 16 * 5)

            def mix(b):
                for m in range(2):
                    for c in range(2):
                        last = nc.tensor.matmul(p_q[:, m * P:(m + 1) * P], wqs[:, c, m * P:(m + 1) * P],
                                                xnT[:, c, bass.ds(b * P, P)], start=(c == 0), stop=(c == 1))
                last.then_inc(q_mm, 1)
                pe.wait_ge(q_feat, b + 1)
                for m in range(2):
                    nc.tensor.matmul(p_l2[:, m * P:(m + 1) * P], kv[:, m, :], qf[:, m, :], start=True, stop=True)
                    last = nc.tensor.matmul(p_l3[:, m * P:(m + 1) * P], ks[:, m, :], qf[:, m, :], start=True, stop=True)
                last.then_inc(q_att, 1)
                pe.wait_ge(q_o, 2 * b + 2)
                after(pe, q_done, b)
                for c in range(2):
                    nc.tensor.matmul(p_o[:, 0:D], oT[:, c, :], wos[:, c, :], start=(c == 0), stop=False)
                nc.tensor.matmul(p_o[:, 0:D], ones[0:1, :], bos[0:1, :], start=False, stop=True).then_inc(q_mix, 1)

            rounds(pe, B, mix)
            pe.wait_ge(x_load, 48)
            with pe.Fori(0, B) as b:
                pe.wait_ge(x_xn, b + 1)
                nc.tensor.transpose(p_t[:, 0:P], xn[:, 0:P], ident[:])
                nc.tensor.transpose(p_t[:, P:D], xn[:, P:D], ident[:]).then_inc(x_tp, 1)
                pe.wait_ge(x_xt, b + 1)
                nc.tensor.matmul(p_g[:, 0:HE], xt[:, 0, :], Wg[:, 0, :], start=True, stop=False)
                nc.tensor.matmul(p_g[:, 0:HE], xt[:, 1, :], Wg[:, 1, :], start=False, stop=True).then_inc(x_h, 1)

    with ExitStack() as c4:
        def sb4(name, shape, dt=F32):
            return c4.enter_context(nc.sbuf_tensor(name, shape, dt))

        def sem4(name):
            return c4.enter_context(nc.semaphore(name))

        NQ = T2 // Q
        S = 3 * HEADS
        idx = sb4("m_idx", [P, G], I32)
        local = sb4("m_local", [P, G])
        rowsg = sb4("m_rows", [P, G, RW])
        parts = sb4("m_parts", [P, STEPS, P], BF16)
        far = sb4("m_far", [P, G, P], BF16)
        wide = sb4("m_wide", [Q * S, STEPS, HEADS, P], BF16)
        of_head = sb4("m_of_head", [Q * S, HEADS])
        of_tile = sb4("m_of_tile", [Q * S, Q])
        take = sb4("m_take", [Q * S, Q, P], BF16)
        minus = sb4("m_minus", [P, HEADS, P], BF16)
        best = sb4("m_best", [P, G, HEADS])
        p_T = [c4.enter_context(nc.psum_tensor(f"m_T{j}", [P, 1024], BF16)) for j in range(2)]
        p_max = [c4.enter_context(nc.psum_tensor(f"m_max{j}", [P, 512], F32)) for j in range(Q)]
        gath = [sem4(f"m_gath{s}") for s in range(STEPS)]
        m_idx, m_local, m_kept, m_parts, m_T, m_wide, m_far, m_mm, m_best, m_max, m_const = (
            sem4(n) for n in ("m_idx_ready", "m_local_ready", "m_kept", "m_parts_ready", "m_T_ready", "m_wide_ready",
                              "m_far_ready", "m_mm", "m_best_ready", "m_max_ready", "m_const"))
        block = c4.enter_context(nc.Block())

        @block.scalar
        def _(act):
            def step(i, s):
                if now := behind(i, s, 0, NQ):
                    r, k = now
                    after(act, gath[k], r * (16 * Q))
                    nc.scalar.copy(idx[:, k * Q:(k + 1) * Q],
                                   list2[:, bass.ds((r * STEPS + k) * Q, Q), 0]).then_inc(m_idx, 1)
                if now := behind(i, s, 2, NQ):
                    r, k = now
                    n = r * STEPS + k
                    rows = slice(k * Q, (k + 1) * Q)
                    act.wait_ge(gath[k], r * (16 * Q) + 16 * Q)
                    after(act, m_T, n - STEPS + 1)
                    nc.scalar.copy(parts[:, k, 0:Q * S].rearrange("p (j c) -> p j c", j=Q),
                                   rowsg[:, rows, 0:S]).then_inc(m_parts, 1)
                    nc.scalar.copy(gat[:, bass.ds(n * Q, Q), :], rowsg[:, rows, S:RW]).then_inc(m_kept, 1)
                    after(act, m_far, (n - STEPS + 1) * Q)
                    nc.scalar.copy(local[:, rows], list2[:, bass.ds(n * Q, Q), 1]).then_inc(m_local, 1)
                    act.wait_ge(m_local, n + 1)
                    after(act, m_mm, (n - STEPS + 1) * Q)
                    for j in range(k * Q, (k + 1) * Q):
                        nc.scalar.activation(far[:, j, :], laneb[:], ACT.Abs, bias=local[:, j:j + 1],
                                             scale=-1.0).then_inc(m_far, 1)
                if now := behind(i, s, 3, NQ):
                    r, k = now
                    n = r * STEPS + k
                    act.wait_ge(m_T, n + 1)
                    after(act, m_mm, (n - STEPS + 1) * Q)
                    for h in range(HEADS):
                        nc.scalar.activation(wide[:, k, h, :], p_T[k % 2][0:Q * S, 0:P], ACT.Copy,
                                             scale=of_head[:, h:h + 1]).then_inc(m_wide, 1)

            act.wait_ge(m_const, 6)
            pipeline(act, NQ, 3, step)

        @block.gpsimd
        def _(pool):
            pool.wait_ge(node_stored, 1)

            def step(i, s):
                n = i * STEPS + s
                pool.wait_ge(m_idx, n + 1)
                after(pool, m_kept, n - STEPS + 1)
                after(pool, turned, turns[0] + n)
                pool.tensor_tensor(turn[:], zero1[:], zero1[:], ALU.add).then_inc(turned, 1)
                for j in range(s * Q, (s + 1) * Q):
                    pool.indirect_dma_start(rowsg[:, j, :], None, node_dram,
                                            bass.IndirectOffsetOnAxis(ap=idx[:, j:j + 1], axis=0)
                                            ).then_inc(gath[s], 16)

            pipeline(pool, NQ, 0, step)
            turns[0] += NQ

        @block.tensor
        def _(pe):
            pe.wait_ge(m_const, 6)

            def step(i, s):
                if now := behind(i, s, 2, NQ):
                    r, k = now
                    n = r * STEPS + k
                    pe.wait_ge(m_parts, n + 1)
                    after(pe, m_wide, (n - 1) * HEADS)
                    nc.tensor.transpose(p_T[k % 2][:, 0:P], parts[:, k, :], identb[:]).then_inc(m_T, 1)
                if now := behind(i, s, 3, NQ):
                    r, k = now
                    n = r * STEPS + k
                    pe.wait_ge(m_far, (n + 1) * Q)
                    pe.wait_ge(m_wide, (n + 1) * HEADS)
                    for j in range(Q):
                        after(pe, m_best, (n - 1) * Q + j + 1)
                        nc.tensor.matmul(p_max[j][:], take[:, j, :], wide[:, k].rearrange("r h n -> r (h n)"),
                                         start=True, stop=False)
                        nc.tensor.matmul(p_max[j][:], far[:, k * Q + j, :], minus[:].rearrange("p h n -> p (h n)"),
                                         start=False, stop=True).then_inc(m_mm, 1)

            pipeline(pe, NQ, 3, step)

        @block.vector
        def _(dve):
            c = Steps(dve, m_const)
            rows = ident[0:Q * S, 0:Q * S]
            c.did(dve.tensor_reduce(of_tile[:], rows.rearrange("r (j c) -> r j c", j=Q), AX.X, ALU.add))
            c.did(dve.tensor_reduce(of_head[:], rows.rearrange("r (j h) -> r h j", h=HEADS), AX.X, ALU.add))
            c.did(dve.tensor_scalar(minus[:], ident[:].unsqueeze(1).broadcast_to([P, HEADS, P]), -FARTHEST, None,
                                    ALU.mult))
            c.settle()
            c.step(dve.tensor_copy(take[:], of_tile[:].unsqueeze(2).broadcast_to([Q * S, Q, P])))
            c.step(dve.memset(parts[:], 0.0))
            dve.nop().then_inc(m_const, 1)

            def step(i, s):
                if now := behind(i, s, 4, NQ):
                    r, k = now
                    n = r * STEPS + k
                    at = places(nc, dve, blk2, n * Q, Q, (B - 1) * SW)
                    for j in range(Q):
                        dve.wait_ge(m_mm, n * Q + j + 1)
                        dve.tensor_reduce(best[:, k * Q + j, :], p_max[j][:].rearrange("p (h n) -> p h n", h=HEADS),
                                          AX.X, ALU.max).then_inc(m_best, 1)
                        if j:
                            maximum(n * Q + j - 1, k * Q + j - 1, at[j - 1])
                    maximum(n * Q + Q - 1, k * Q + Q - 1, at[Q - 1])

            def maximum(t, j, place):
                v = own_flat[:, HEADS:][:, bass.ds(place, HEADS)]
                dve.wait_ge(m_best, t + 1)
                after(dve, m_max, t)
                dve.tensor_tensor(v, v, best[:, j, :], ALU.max).then_inc(m_max, 1)

            pipeline(dve, NQ, 4, step)

    with ExitStack() as c5:
        def sb5(name, shape, dt=F32):
            return c5.enter_context(nc.sbuf_tensor(name, shape, dt))

        def sem5(name):
            return c5.enter_context(nc.semaphore(name))

        local = sb5("s_local", [P, G])
        hot = sb5("s_hot", [P, G, P], BF16)
        hotT = sb5("s_hotT", [P, G, P], BF16)
        z = sb5("s_z", [P, G, HEADS])
        val = sb5("s_val", [P, G, HEADS + HE])
        rest = sb5("s_rest", [P, G, HEADS + HE])
        val3 = sb5("s_val3", [P, G, 3, HEADS + HE], BF16)
        own3 = sb5("s_own3", [P, B * SW], BF16)
        ed = sb5("s_ed", [P, 2, Q, 2 * HEADS])
        part_sum = sb5("s_part_sum", [P, 2, Q, HEADS + HE])
        self_z = sb5("self_z", [P, B, HEADS])
        agg = hotT[:].rearrange("p j n -> p (j n)").bitcast(F32)[:, 0:B * HE].rearrange("p (b w) -> p b w", w=HE)
        sq = hot[:].rearrange("p j n -> p (j n)").bitcast(F32)[:, 0:B * HE].rearrange("p (b w) -> p b w", w=HE)
        mu = sb5("mu", [P, B])
        var = sb5("var", [P, B])
        sc = sb5("sc", [P, B, EXPERTS])
        less = mu
        rank_ = sb5("rank_", [P, B, EXPERTS])
        top = sb5("top", [P, B])
        rowc = sb5("rowc", [P, 3, HE])
        p_T = [c5.enter_context(nc.psum_tensor(f"s_T{j}", [P, 1024], BF16)) for j in range(2)]
        p_e = [c5.enter_context(nc.psum_tensor(f"s_e{j}", [P, 512], F32)) for j in range(2)]
        p_s = [c5.enter_context(nc.psum_tensor(f"s_s{j}", [P, 512], F32)) for j in range(2)]
        s_step, s_hot, s_T, s_hotT, s_e, s_zr, s_exp, s_val, s_mm, s_sum, s_m, s_ld, s_a, s_b = (
            sem5(n) for n in ("s_step", "s_hot_ready", "s_T_ready", "s_hotT_ready", "s_e_ready", "s_z_ready", "s_exp",
                              "s_val_ready", "s_mm", "s_sum", "s_m", "s_ld", "s_a", "s_b"))
        s_local = sem5("s_local_ready")
        s_zs, s_ed, s_high, s_mid, s_low, s_rest, s_part = (
            sem5(n) for n in ("s_zs", "s_ed_ready", "s_high", "s_mid", "s_low", "s_rest_ready", "s_part"))
        NQ = T2 // Q
        block = c5.enter_context(nc.Block())
        K = HEADS + HE
        E3 = 3 * 2 * HEADS

        @block.sync
        def _(sp):
            for n, a in enumerate((b_gat, ln_gamma, ln_beta)):
                sp.dma_start(rowc[:, n, :], a.partition_broadcast(P)).then_inc(s_ld, 16)

        @block.gpsimd
        def _(pool):
            pool.wait_ge(s_m, 1)

            def step(i, s):
                n = i * STEPS + s
                pool.wait_ge(s_local, n + 1)
                after(pool, s_mm, n - STEPS + 1)
                after(pool, turned, turns[0] + n)
                pool.tensor_tensor(turn[:], zero1[:], zero1[:], ALU.add).then_inc(turned, 1)
                for j in range(s * Q, (s + 1) * Q):
                    pool.tensor_scalar(hot[:, j, :], laneb[:], local[:, j:j + 1], None,
                                       ALU.is_equal).then_inc(s_hot, 1)

            pipeline(pool, NQ, 0, step)
            turns[0] += NQ

        @block.tensor
        def _(pe):
            pe.wait_ge(s_m, 1)

            def step(i, s):
                if now := behind(i, s, 1, NQ):
                    r, k = now
                    n = r * STEPS + k
                    pe.wait_ge(s_hotT, n + 1)
                    after(pe, s_ed, n - 1)
                    at = places(nc, pe, blk2, n * Q, Q, (B - 1) * SW)
                    for j in range(Q):
                        mm = nc.tensor.matmul(p_e[k % 2][:, j * E3:(j + 1) * E3], hotT[:, k * Q + j, :],
                                              own3[:, bass.ds(at[j], E3)], start=True, stop=True)
                    mm.then_inc(s_e, 1)
                if now := behind(i, s, 0, NQ):
                    r, k = now
                    n = r * STEPS + k
                    pe.wait_ge(s_hot, (n + 1) * Q)
                    after(pe, s_hotT, n - 1)
                    for j in range(Q):
                        mm = nc.tensor.transpose(p_T[k % 2][:, j * P:(j + 1) * P], hot[:, k * Q + j, :], identb[:])
                    mm.then_inc(s_T, 1)
                if now := behind(i, s, 3, NQ):
                    r, k = now
                    n = r * STEPS + k
                    pe.wait_ge(s_low, n + 1)
                    pe.wait_ge(s_mid, n + 1)
                    after(pe, s_part, n - 1)
                    for j in range(Q):
                        mm = nc.tensor.matmul(p_s[k % 2][:, j * 3 * K:(j + 1) * 3 * K], hot[:, k * Q + j, :],
                                              val3[:, k * Q + j].rearrange("p c w -> p (c w)"), start=True, stop=True)
                    mm.then_inc(s_mm, 1)

            pipeline(pe, NQ, 3, step)

        @block.scalar
        def _(act):
            act.wait_ge(s_a, 1)
            nc.scalar.activation(asum[:, :, 0:HEADS], self_z[:], ACT.Exp).then_inc(s_b, 1)

            def copy_local(r, k):
                after(act, s_hot, r * G + (k + 1) * Q - G)
                nc.scalar.copy(local[:, k * Q:(k + 1) * Q],
                               list2[:, bass.ds(r * G + k * Q, Q), 1]).then_inc(s_local, 1)

            def step(i, s):
                if now := behind(i, s, 2, NQ):
                    r, k = now
                    n = r * STEPS + k
                    act.wait_ge(s_zr, n + 1)
                    nc.scalar.activation(val[:, k * Q:(k + 1) * Q, 0:HEADS], z[:, k * Q:(k + 1) * Q, :],
                                         ACT.Exp).then_inc(s_exp, 1)
                if now := behind(i, s, 3, NQ):
                    r, k = now
                    n = r * STEPS + k
                    act.wait_ge(s_rest, n + 1)
                    nc.scalar.copy(val3[:, k * Q:(k + 1) * Q, 1, :], rest[:, k * Q:(k + 1) * Q, :]).then_inc(s_mid, 1)
                if now := behind(i, s, 2, NQ):
                    r, k = now
                    n = r * STEPS + k
                    act.wait_ge(s_val, n + 1)
                    after(act, s_mm, n - STEPS + 1)
                    nc.scalar.copy(val3[:, k * Q:(k + 1) * Q, 0, :], val[:, k * Q:(k + 1) * Q, :]).then_inc(s_high, 1)
                if now := behind(i, s, 0, NQ):
                    r, k = now
                    n = r * STEPS + k
                    act.wait_ge(s_T, n + 1)
                    after(act, s_e, n - STEPS + 1)
                    nc.scalar.copy(hotT[:, k * Q:(k + 1) * Q, :].rearrange("p j n -> p (j n)"),
                                   p_T[k % 2][:, 0:Q * P]).then_inc(s_hotT, 1)
                    copy_local(r + 1, k)

            for k in range(STEPS):
                copy_local(0, k)
            pipeline(act, NQ, 3, step)
            act.wait_ge(s_a, 2)
            nc.scalar.activation(var[:], var[:], ACT.Sqrt, bias=epsc[:, 0:1]).then_inc(s_b, 1)
            act.wait_ge(s_a, 3)
            nc.scalar.activation(gate[:], sc[:], ACT.Exp).then_inc(s_b, 1)

        @block.vector
        def _(dve):
            s = Steps(dve, s_step)
            self_z8 = sq.rearrange("p b w -> p (b w)")[:, 0:B * 2 * HEADS].rearrange("p (b w) -> p b w", w=2 * HEADS)
            mx = vmax
            s.step(dve.tensor_copy(own[:, :, 0:HEADS], node[:, :, A_D:A_D + HEADS]))
            s.step(dve.tensor_tensor(mx, mx, node[:, :, A_D:A_D + HEADS], ALU.add))
            s.step(dve.scalar_tensor_tensor(out=mx, in0=mx, scalar=0.2, in1=mx, op0=ALU.mult, op1=ALU.max))
            o3 = own3[:].rearrange("p (b w) -> p b w", w=SW)
            left = own[:, :, 0:2 * HEADS]
            for c in range(3):
                part = o3[:, :, c * 2 * HEADS:(c + 1) * 2 * HEADS]
                s.step(dve.tensor_copy(part, left))
                if c < 2:
                    s.step(dve.tensor_tensor(self_z8, left, part, ALU.subtract))
                    left = self_z8
            dve.nop().then_inc(s_m, 1)
            s.step(dve.tensor_tensor(self_z[:], node[:, :, A_S:A_S + HEADS], node[:, :, A_D:A_D + HEADS], ALU.add))
            s.step(dve.scalar_tensor_tensor(out=self_z[:], in0=self_z[:], scalar=0.2, in1=self_z[:],
                                            op0=ALU.mult, op1=ALU.max))
            s.step(dve.tensor_tensor(self_z[:], self_z[:], mx, ALU.subtract))
            s.step(dve.tensor_scalar(self_z[:], self_z[:], 0.0, None, ALU.min))
            dve.nop().then_inc(s_a, 1)
            dve.wait_ge(s_b, 1)
            for k in range(HEADS):
                e = slice(HEADS + k * EXPERTS, HEADS + (k + 1) * EXPERTS)
                s.did(dve.tensor_tensor(asum[:, :, e], node[:, :, H0 + k * EXPERTS:H0 + (k + 1) * EXPERTS],
                                        asum[:, :, k:k + 1].broadcast_to([P, B, EXPERTS]), ALU.mult))
            s.settle()

            def step(i, s):
                if now := behind(i, s, 3, NQ):
                    r, k = now
                    n = r * STEPS + k
                    vs = val[:, k * Q:(k + 1) * Q, :]
                    dve.wait_ge(s_high, n + 1)
                    dve.tensor_tensor(rest[:, k * Q:(k + 1) * Q, :], vs, val3[:, k * Q:(k + 1) * Q, 0, :],
                                      ALU.subtract).then_inc(s_rest, 1)
                if now := behind(i, s, 2, NQ):
                    r, k = now
                    n = r * STEPS + k
                    dve.wait_ge(s_exp, n + 1)
                    vs = val[:, k * Q:(k + 1) * Q, :]
                    dve.tensor_tensor(vs[:, :, HEADS:K].rearrange("p j (h e) -> p j h e", h=HEADS),
                                      gat[:, bass.ds(n * Q, Q), HEADS:K].rearrange("p j (h e) -> p j h e", h=HEADS),
                                      vs[:, :, 0:HEADS].unsqueeze(3).broadcast_to([P, Q, HEADS, EXPERTS]),
                                      ALU.mult).then_inc(s_val, 1)
                if now := behind(i, s, 4, NQ):
                    r, k = now
                    n = r * STEPS + k
                    dve.wait_ge(s_mm, n + 1)
                    after(dve, s_sum, (n - 1) * Q)
                    dve.tensor_reduce(part_sum[:, k % 2], p_s[k % 2][:, 0:Q * 3 * K].rearrange(
                        "p (j c w) -> p j w c", j=Q, c=3), AX.X, ALU.add).then_inc(s_part, 1)
                    dve.wait_ge(s_part, n + 1)
                    at = places(nc, dve, blk2, n * Q, Q, (B - 1) * SW)
                    for j in range(Q):
                        t = n * Q + j
                        a = own_flat[:, 2 * HEADS:][:, bass.ds(at[j], K)]
                        after(dve, s_sum, t)
                        dve.tensor_tensor(a, a, part_sum[:, k % 2, j, :], ALU.add).then_inc(s_sum, 1)
                if now := behind(i, s, 3, NQ):
                    r, k = now
                    n = r * STEPS + k
                    dve.wait_ge(s_mid, n + 1)
                    dve.tensor_tensor(val3[:, k * Q:(k + 1) * Q, 2, :], rest[:, k * Q:(k + 1) * Q, :],
                                      val3[:, k * Q:(k + 1) * Q, 1, :], ALU.subtract).then_inc(s_low, 1)
                if now := behind(i, s, 1, NQ):
                    r, k = now
                    n = r * STEPS + k
                    zs = z[:, k * Q:(k + 1) * Q, :]
                    pe_ = ed[:, k % 2]
                    dve.wait_ge(s_e, n + 1)
                    dve.tensor_reduce(pe_, p_e[k % 2][:, 0:Q * E3].rearrange("p (j c w) -> p j w c", j=Q, c=3),
                                      AX.X, ALU.add).then_inc(s_ed, 1)
                    dve.wait_ge(s_ed, n + 1)
                    after(dve, s_exp, n - STEPS + 1)
                    dve.tensor_tensor(zs, gat[:, bass.ds(n * Q, Q), 0:HEADS], pe_[:, :, 0:HEADS],
                                      ALU.add).then_inc(s_zs, 1)
                    dve.wait_ge(s_zs, n * 3 + 1)
                    dve.scalar_tensor_tensor(out=zs, in0=zs, scalar=0.2, in1=zs, op0=ALU.mult,
                                             op1=ALU.max).then_inc(s_zs, 1)
                    dve.wait_ge(s_zs, n * 3 + 2)
                    dve.tensor_tensor(zs, zs, pe_[:, :, HEADS:2 * HEADS], ALU.subtract).then_inc(s_zs, 1)
                    dve.wait_ge(s_zs, n * 3 + 3)
                    dve.tensor_scalar(zs, zs, 0.0, None, ALU.min).then_inc(s_zr, 1)

            pipeline(dve, NQ, 4, step)
            dve.wait_ge(s_sum, T2)
            s.step(dve.tensor_scalar(asum[:, :, 0:HEADS], asum[:, :, 0:HEADS], 1e-16, None, ALU.add))
            s.step(dve.reciprocal(asum[:, :, 0:HEADS], asum[:, :, 0:HEADS]))
            for k in range(HEADS):
                s.did(dve.tensor_tensor(agg[:, :, k * EXPERTS:(k + 1) * EXPERTS],
                                        asum[:, :, HEADS + k * EXPERTS:HEADS + (k + 1) * EXPERTS],
                                        asum[:, :, k:k + 1].broadcast_to([P, B, EXPERTS]), ALU.mult))
            dve.wait_ge(s_ld, 48)
            s.settle()

            def row(n):
                return rowc[:, n, :].unsqueeze(1).broadcast_to([P, B, HE])

            def wide(v):
                return v[:].unsqueeze(2).broadcast_to([P, B, HE])

            s.step(dve.tensor_tensor(agg, agg, row(0), ALU.add))
            s.step(dve.tensor_reduce(mu[:], agg, AX.X, ALU.add))
            s.step(dve.tensor_scalar(mu[:], mu[:], 1.0 / HE, None, ALU.mult))
            s.step(dve.tensor_tensor(agg, agg, wide(mu), ALU.subtract))
            s.step(dve.tensor_tensor(sq, agg, agg, ALU.mult))
            s.step(dve.tensor_reduce(var[:], sq, AX.X, ALU.add))
            s.step(dve.tensor_scalar(var[:], var[:], 1.0 / HE, None, ALU.mult))
            dve.nop().then_inc(s_a, 1)
            dve.wait_ge(s_b, 2)
            s.step(dve.reciprocal(var[:], var[:]))
            s.step(dve.tensor_tensor(agg, agg, wide(var), ALU.mult))
            s.step(dve.tensor_tensor(agg, agg, row(1), ALU.mult))
            s.step(dve.tensor_tensor(agg, agg, row(2), ALU.add))
            s.step(dve.tensor_reduce(sc[:], agg.rearrange("p b (h e) -> p b e h", h=HEADS), AX.X, ALU.add))
            s.step(dve.tensor_scalar(sc[:], sc[:], 1.0 / HEADS, None, ALU.mult))
            s.step(dve.memset(rank_[:], 0.0))
            for a in range(EXPERTS):
                for o in range(EXPERTS):
                    if o != a:
                        s.step(dve.tensor_tensor(less[:], sc[:, :, o], sc[:, :, a], ALU.is_ge if o < a else ALU.is_gt))
                        s.step(dve.tensor_tensor(rank_[:, :, a], rank_[:, :, a], less[:], ALU.add))
            s.step(dve.tensor_reduce(top[:], sc[:], AX.X, ALU.max))
            s.step(dve.tensor_tensor(sc[:], sc[:], top[:].unsqueeze(2).broadcast_to([P, B, EXPERTS]), ALU.subtract))
            dve.nop().then_inc(s_a, 1)
            s.step(dve.tensor_scalar(rank_[:], rank_[:], 2.0, None, ALU.is_lt))
            dve.wait_ge(s_b, 3)
            s.step(dve.tensor_tensor(gate[:], gate[:], rank_[:], ALU.mult))
            s.step(dve.tensor_reduce(top[:], gate[:], AX.X, ALU.add))
            s.step(dve.reciprocal(top[:], top[:]))
            s.step(dve.tensor_tensor(gate[:], gate[:], top[:].unsqueeze(2).broadcast_to([P, B, EXPERTS]), ALU.mult))

    with ExitStack() as c6:
        def sem6(name):
            return c6.enter_context(nc.semaphore(name))

        def ps6(name):
            return c6.enter_context(nc.psum_tensor(name, [P, 512], F32))

        at = [0]

        def part(*shape):
            n = 1
            for v in shape:
                n *= v
            v = big[:, at[0]:at[0] + n]
            at[0] += n
            return v

        TG = 4
        W1 = part(EXPERTS * 2 * FH).rearrange("p (e c n) -> p e c n", e=EXPERTS, c=2)
        W2 = part(EXPERTS * FC * D).rearrange("p (e f n) -> p e f n", e=EXPERTS, f=FC)
        b1c = part(EXPERTS * FC)
        xn = part(TG * D).rearrange("p (t d) -> p t d", t=TG)
        xt = part(2 * TG * P).rearrange("p (c n) -> p c n", c=2)
        hT = part(2 * FC * TG * P).rearrange("p (w f n) -> p w f n", w=2, f=FC)
        b2r = part(EXPERTS * D).rearrange("p (e d) -> p e d", e=EXPERTS)
        p_t = [ps6("f_t0"), ps6("f_t1")]
        p_h = [ps6("f_h0"), ps6("f_h1")]
        p_y = [ps6(f"f_y{j}") for j in range(TG)]
        f_ld, f_xn, f_tp, f_xt, f_h, f_g, f_y, f_add, f_bias, f_out = (
            sem6(n) for n in ("f_ld", "f_xn", "f_tp", "f_xt", "f_h", "f_g", "f_y", "f_add", "f_bias", "f_out"))
        n_group = FULL // TG
        assert n_group * TG == FULL and LAST
        block = c6.enter_context(nc.Block())

        @block.sync
        def _(sp):
            for e in range(EXPERTS):
                sp.dma_start(W1[:, e], fW1[e].rearrange("(c p) n -> p c n", p=P)).then_inc(f_ld, 16)
                sp.dma_start(W2[:, e], fW2[e].rearrange("(f p) n -> p f n", p=P)).then_inc(f_ld, 16)
                for f in range(FC):
                    sp.dma_start(b1c[:, e * FC + f:e * FC + f + 1],
                                 fb1[e, f * P:(f + 1) * P].rearrange("(p o) -> p o", o=1)).then_inc(f_ld, 16)
            for e in range(EXPERTS):
                sp.dma_start(b2r[:, e, :], fb2[e].partition_broadcast(P)).then_inc(f_ld, 16)
            with sp.Fori(0, n_group) as g:
                sp.wait_ge(f_add, g * (EXPERTS * TG) + EXPERTS * TG)
                sp.dma_start(out[bass.ds(g * (TG * P), TG * P), :].rearrange("(t p) d -> p t d", p=P),
                             res[:, bass.ds(g * TG, TG), :]).then_inc(f_out, 16)
            sp.wait_ge(f_add, n_group * EXPERTS * TG + EXPERTS)
            sp.dma_start(out[FULL * P:, :], res[0:LAST, FULL, :]).then_inc(f_out, 16)
            sp.wait_ge(f_out, 16 * (n_group + 1))

        N_LD = 16 * EXPERTS * (3 + FC)

        def over_groups(eng, body):
            rounds(eng, n_group, lambda g: body(g, TG))
            body(n_group, 1)

        @block.vector
        def _(dve):
            dve.wait_ge(f_ld, N_LD)

            def body(g, nt):
                for t in range(nt):
                    after(dve, f_tp, g)
                    dve.tensor_scalar(xn[:, t, :], res[:, bass.ds(g * TG + t, 1), :].rearrange("p o d -> p (o d)"),
                                      mean[:, bass.ds(g * TG + t, 1), 0:1].rearrange("p o w -> p (o w)"),
                                      rstd[:, bass.ds(g * TG + t, 1)], ALU.subtract, ALU.mult).then_inc(f_xn, 1)
                for e in range(EXPERTS):
                    for t in range(nt):
                        b = g * TG + t
                        r = res[:, bass.ds(b, 1), :].rearrange("p o d -> p (o d)")
                        if e:
                            dve.wait_ge(f_bias, g * (EXPERTS * TG) + (e - 1) * nt + t + 1)
                        else:
                            dve.wait_ge(f_xn, g * TG + nt)
                        dve.scalar_tensor_tensor(out=r, in0=b2r[:, e, :],
                                                 scalar=gate[:, bass.ds(b, 1), e:e + 1].rearrange("p o w -> p (o w)"),
                                                 in1=r, op0=ALU.mult, op1=ALU.add).then_inc(f_bias, 1)
                for e in range(EXPERTS):
                    for t in range(nt):
                        b = g * TG + t
                        r = res[:, bass.ds(b, 1), :].rearrange("p o d -> p (o d)")
                        n = g * (EXPERTS * TG) + e * nt + t + 1
                        dve.wait_ge(f_y, n)
                        if e:
                            dve.wait_ge(f_add, n - nt)
                        else:
                            dve.wait_ge(f_bias, (g + 1) * (EXPERTS * TG) if nt == TG else g * (EXPERTS * TG) + EXPERTS)
                        dve.scalar_tensor_tensor(out=r, in0=p_y[t][:, 0:D],
                                                 scalar=gate[:, bass.ds(b, 1), e:e + 1].rearrange("p o w -> p (o w)"),
                                                 in1=r, op0=ALU.mult, op1=ALU.add).then_inc(f_add, 1)

            over_groups(dve, body)

        @block.scalar
        def _(act):
            act.wait_ge(f_ld, N_LD)

            def body(g, nt):
                act.wait_ge(f_tp, g + 1)
                for c in range(2):
                    nc.scalar.copy(xt[:, c, 0:nt * P], p_t[c][:, 0:nt * P]).then_inc(f_xt, 1)
                for e in range(EXPERTS):
                    for f in range(FC):
                        n = g * (EXPERTS * FC) + e * FC + f + 1
                        act.wait_ge(f_h, n)
                        if e >= 2:
                            act.wait_ge(f_y, g * (EXPERTS * TG) + (e - 1) * nt)
                        nc.scalar.activation(hT[:, e % 2, f, 0:nt * P], p_h[f % 2][:, 0:nt * P], ACT.Gelu,
                                             bias=b1c[:, e * FC + f:e * FC + f + 1]).then_inc(f_g, 1)

            over_groups(act, body)

        @block.tensor
        def _(pe):
            pe.wait_ge(f_ld, N_LD)

            def body(g, nt):
                pe.wait_ge(f_xn, g * TG + nt)
                after(pe, f_y, g * (EXPERTS * TG))
                for c in range(2):
                    for t in range(nt):
                        mm = nc.tensor.transpose(p_t[c][:, t * P:(t + 1) * P], xn[:, t, c * P:(c + 1) * P], ident[:])
                mm.then_inc(f_tp, 1)
                pe.wait_ge(f_xt, 2 * g + 2)

                def up(e):
                    for f in range(FC):
                        n = g * (EXPERTS * FC) + e * FC + f
                        if e or f >= 2:
                            pe.wait_ge(f_g, n - 1)
                        for c in range(2):
                            mm = nc.tensor.matmul(p_h[f % 2][:, 0:nt * P], W1[:, e, c, f * P:(f + 1) * P],
                                                  xt[:, c, 0:nt * P], start=(c == 0), stop=(c == 1))
                        mm.then_inc(f_h, 1)

                def down(e):
                    pe.wait_ge(f_g, g * (EXPERTS * FC) + (e + 1) * FC)
                    for t in range(nt):
                        if e:
                            pe.wait_ge(f_add, g * (EXPERTS * TG) + (e - 1) * nt + t + 1)
                        else:
                            after(pe, f_add, g * (EXPERTS * TG))
                        for f in range(FC):
                            mm = nc.tensor.matmul(p_y[t][:, 0:D], hT[:, e % 2, f, t * P:(t + 1) * P], W2[:, e, f, :],
                                             start=(f == 0), stop=(f == FC - 1))
                        mm.then_inc(f_y, 1)

                up(0)
                for e in range(1, EXPERTS):
                    up(e)
                    down(e - 1)
                down(EXPERTS - 1)

            over_groups(pe, body)

    ctx.close()


_INS = ['x', 'src', 'dst', 'L0_gnn_W1', 'L0_gnn_b1', 'L0_gnn_W2', 'L0_gnn_b2', 'L0_mix_wq', 'L0_mix_bq', 'L0_mix_wk',
        'L0_mix_bk', 'L0_mix_wv', 'L0_mix_bv', 'L0_mix_wo', 'L0_mix_bo', 'L0_ffn_W_gat', 'L0_ffn_att_src',
        'L0_ffn_att_dst', 'L0_ffn_b_gat', 'L0_ffn_ln_gamma', 'L0_ffn_ln_beta', 'L0_ffn_W1', 'L0_ffn_b1', 'L0_ffn_W2',
        'L0_ffn_b2', 'L0_ffn_edge_index']


def kernel(**inputs):
    import numpy as _np
    import concourse.bacc as _bacc
    from concourse import mybir as _mybir
    from concourse.bass_utils import run_bass_kernel_spmd as _run

    nc = _bacc.Bacc("TRN2", target_bir_lowering=False, num_devices=1)
    arrays, args = {}, []
    for name in _INS:
        a = _np.ascontiguousarray(inputs[name])
        arrays[f"in_{name}_dram"] = a
        args.append(nc.dram_tensor(f"in_{name}_dram", a.shape, _mybir.dt.from_np(a.dtype), kind="ExternalInput").ap())
    args.append(nc.dram_tensor("out_0_dram", inputs["x"].shape, F32, kind="ExternalOutput").ap())
    gps_kernel(nc, *args)
    r = _run(nc, [arrays], core_ids=[0])
    return r.results[0]["out_0_dram"]
```
